# Optimizing a Trainium2 kernel written in Bass

```python
import numpy as np
import jax
import jax.numpy as jnp

def _softmax(x, axis=-1):
    return jax.nn.softmax(x, axis=axis)

def _gelu(x):
    return jax.nn.gelu(x, approximate=True)

def _silu(x):
    return jax.nn.silu(x)

def _sigmoid(x):
    return jax.nn.sigmoid(x)

def _layernorm(x, axis=-1, eps=1e-05):
    m = jnp.mean(x, axis=axis, keepdims=True)
    v = jnp.var(x, axis=axis, keepdims=True)
    return (x - m) / jnp.sqrt(v + eps)

def _scatter_add(tgt, idx, src, axis=0):
    return tgt.at[idx].add(src)

def _segment_sum(src, seg, n):
    return jax.ops.segment_sum(src, seg, n)
kernel_name = 'mk_gps_d1_gnn_r8_09990e'

def setup_inputs(seed: int=0):
    np.random.seed(seed)
    _w = jnp.asarray

    def _rec_inputs():
        import jax
        import jax.numpy as jnp
        _gk = jax.random.key(seed)
        x = -0.0003713 + 1 * jax.random.normal(jax.random.fold_in(_gk, 1), (6250, 256), jnp.float32)
        src = jax.random.randint(jax.random.fold_in(_gk, 2), (100000,), 0, 6250, jnp.int32)
        dst = jnp.minimum((6250 * jax.random.uniform(jax.random.fold_in(_gk, 3), (100000,)) ** 2.0).astype(jnp.int32), 49999)
        _o = jnp.argsort(dst, stable=True)
        src = src[_o]
        dst = dst[_o]
        return (x, src, dst)
    x, src, dst = _rec_inputs()

    def _L0_gnn_setup():
        import jax, jax.numpy as jnp
        import numpy as np
        N = 6250
        E = 200000
        D = 256
        H = 256
        EPS = 1e-05

        def _gnn_layer(x, row, col, W, b, g, beta):
            n = x.shape[0]
            neigh = x[col]
            agg = jax.ops.segment_sum(neigh, row, num_segments=n)
            deg = jax.ops.segment_sum(jnp.ones((row.shape[0],), x.dtype), row, num_segments=n)
            deg = jnp.maximum(deg, 1.0)[:, None]
            h = (x + agg / deg) @ W.T + b
            mu = jnp.mean(h, axis=-1, keepdims=True)
            var = jnp.mean(jnp.square(h - mu), axis=-1, keepdims=True)
            hn = (h - mu) * jax.lax.rsqrt(var + EPS) * g + beta
            return jax.nn.silu(hn)
        key = jax.random.key(seed)
        ks = jax.random.split(key, 12)
        x = jax.random.normal(ks[0], (N, D), dtype=jnp.float32)
        edge_index = jax.random.randint(ks[1], (2, E), 0, N, dtype=jnp.int32)
        s0 = 1.0 / np.sqrt(D)
        s1 = 1.0 / np.sqrt(H)
        W0 = jax.random.uniform(ks[2], (H, D), jnp.float32, -s0, s0)
        b0 = jax.random.uniform(ks[3], (H,), jnp.float32, -s0, s0)
        g0 = jnp.ones((H,), jnp.float32)
        beta0 = jnp.zeros((H,), jnp.float32)
        W1 = jax.random.uniform(ks[4], (H, H), jnp.float32, -s1, s1)
        b1 = jax.random.uniform(ks[5], (H,), jnp.float32, -s1, s1)
        g1 = jnp.ones((H,), jnp.float32)
        beta1 = jnp.zeros((H,), jnp.float32)
        return {'x': x, 'edge_index': edge_index, 'W0': W0, 'b0': b0, 'g0': g0, 'beta0': beta0, 'W1': W1, 'b1': b1, 'g1': g1, 'beta1': beta1}
    _L0_gnn_all = _L0_gnn_setup()
    _L0_gnn_in = {k: v for k, v in _L0_gnn_all.items() if k in ('W0', 'b0', 'g0', 'beta0', 'W1', 'b1', 'g1', 'beta1')}
    del _L0_gnn_all

    def _L0_mix_setup():
        import jax, jax.numpy as jnp
        import numpy as np
        C_CURV = 1.0
        MIN_NORM = 1e-15
        BALL_EPS = 1e-05
        ATT_EPS = 1e-15
        DIM = 32

        def _norm(x):
            return jnp.clip(jnp.linalg.norm(x, axis=-1, keepdims=True), MIN_NORM)

        def proj(x, c):
            maxnorm = (1.0 - BALL_EPS) / jnp.sqrt(c)
            n = _norm(x)
            return jnp.where(n > maxnorm, x / n * maxnorm, x)

        def expmap0(u, c):
            sc = jnp.sqrt(c)
            n = _norm(u)
            return jnp.tanh(sc * n) * u / (sc * n)

        def logmap0(p, c):
            sc = jnp.sqrt(c)
            n = _norm(p)
            return jnp.arctanh(jnp.clip(sc * n, -1.0 + 1e-07, 1.0 - 1e-07)) * p / (sc * n)

        def mobius_add(x, y, c):
            x2 = jnp.sum(x * x, -1, keepdims=True)
            y2 = jnp.sum(y * y, -1, keepdims=True)
            xy = jnp.sum(x * y, -1, keepdims=True)
            num = (1 + 2 * c * xy + c * y2) * x + (1 - c * x2) * y
            den = 1 + 2 * c * xy + c * c * x2 * y2
            return num / jnp.clip(den, MIN_NORM)

        def conv1d(x, w, pad, groups=1):
            return jax.lax.conv_general_dilated(x, w, (1,), [(pad, pad)], dimension_numbers=('NCH', 'OIH', 'NCH'), feature_group_count=groups)

        def batchnorm(x, gamma, beta):
            mean = jnp.mean(x, axis=(0, 2), keepdims=True)
            var = jnp.var(x, axis=(0, 2), keepdims=True)
            xn = (x - mean) * jax.lax.rsqrt(var + 1e-05)
            return gamma[None, :, None] * xn + beta[None, :, None]

        def _reference_tuple_inner(x, w_qkv, bn_gamma, bn_beta, w_dw, w_pw, w_res, b_res):
            c = C_CURV
            h = logmap0(proj(x, c), c)
            h = jnp.transpose(h, (1, 2, 0))
            h = conv1d(h, w_qkv, pad=2)
            h = batchnorm(h, bn_gamma, bn_beta)
            h = jax.nn.relu(jnp.transpose(h, (2, 0, 1)))
            qkv = proj(expmap0(h, c), c)
            t = jnp.transpose(logmap0(proj(qkv, c), c), (1, 2, 0))
            s = conv1d(t, w_dw, pad=2, groups=t.shape[1])
            s = conv1d(s, w_pw, pad=0, groups=t.shape[1] // DIM)
            cat = jnp.concatenate([t, s], axis=1)
            ai = proj(expmap0(jnp.transpose(cat, (2, 0, 1)), c), c)
            t2 = logmap0(proj(ai, c), c)
            L, N, C2 = t2.shape
            g = C2 // (3 * DIM)
            qkv3 = jnp.transpose(t2, (1, 2, 0)).reshape(N, g, 3 * DIM, L)
            q, k, v = jnp.split(qkv3, 3, axis=2)
            q = jax.nn.relu(q)
            k = jax.nn.relu(k)
            vk = jnp.einsum('ngdl,ngel->ngde', v, k)
            out = jnp.einsum('ngde,ngdl->ngdl', vk, q)
            out = out / (jnp.sum(v, -1, keepdims=True) + ATT_EPS)
            out = jnp.transpose(out.reshape(N, g * DIM, L), (2, 0, 1))
            fx_h = proj(expmap0(out, c), c)
            ft = jnp.transpose(logmap0(proj(fx_h, c), c), (1, 2, 0))
            ft = conv1d(ft, w_res, pad=0) + b_res[None, :, None]
            fx = proj(expmap0(jnp.transpose(ft, (2, 0, 1)), c), c)
            residual = mobius_add(fx, x, c)
            return (fx, residual)
        key = jax.random.key(seed)
        ks = jax.random.split(key, 6)
        L, N, C, TD = (256, 16, 256, 256)
        x = jax.random.normal(ks[0], (L, N, C), jnp.float32) * 0.05
        w_qkv = jax.random.normal(ks[1], (3 * TD, C, 5), jnp.float32) / np.sqrt(C * 5)
        bn_gamma = jnp.ones((3 * TD,), jnp.float32)
        bn_beta = jnp.zeros((3 * TD,), jnp.float32)
        w_dw = jax.random.normal(ks[2], (3 * TD, 1, 5), jnp.float32) / np.sqrt(5.0)
        w_pw = jax.random.normal(ks[3], (3 * TD, DIM, 1), jnp.float32) / np.sqrt(DIM)
        w_res = jax.random.normal(ks[4], (C, 2 * TD, 1), jnp.float32) / np.sqrt(2 * TD)
        b_res = jnp.zeros((C,), jnp.float32)
        return {'x': x, 'w_qkv': w_qkv, 'bn_gamma': bn_gamma, 'bn_beta': bn_beta, 'w_dw': w_dw, 'w_pw': w_pw, 'w_res': w_res, 'b_res': b_res}
    _L0_mix_all = _L0_mix_setup()
    _L0_mix_in = {k: v for k, v in _L0_mix_all.items() if k in ('w_qkv', 'bn_gamma', 'bn_beta', 'w_dw', 'w_pw', 'w_res', 'b_res')}
    del _L0_mix_all

    def _L0_ffn_setup():
        import jax, jax.numpy as jnp
        import numpy as np
        DIM = 256
        H = 8
        D = 64
        G = 64
        INNER = H * D
        SCALE = D ** (-0.5)
        key = jax.random.key(seed)
        ks = jax.random.split(key, 12)
        B, N = (4, 2048)
        x = jax.random.normal(ks[0], (B, N, DIM), dtype=jnp.float32)
        s = lambda fan_in: 1.0 / np.sqrt(fan_in)
        W_fx = jax.random.normal(ks[1], (DIM, INNER), dtype=jnp.float32) * s(DIM)
        b_fx = jnp.zeros((INNER,), dtype=jnp.float32)
        W_x = jax.random.normal(ks[2], (DIM, INNER), dtype=jnp.float32) * s(DIM)
        b_x = jnp.zeros((INNER,), dtype=jnp.float32)
        A = jax.random.normal(ks[3], (G, D), dtype=jnp.float32)
        Q, _ = jnp.linalg.qr(A.T)
        W_slice = Q[:, :G].astype(jnp.float32)
        b_slice = jnp.zeros((G,), dtype=jnp.float32)
        W_q = jax.random.normal(ks[4], (D, D), dtype=jnp.float32) * s(D)
        W_k = jax.random.normal(ks[5], (D, D), dtype=jnp.float32) * s(D)
        W_v = jax.random.normal(ks[6], (D, D), dtype=jnp.float32) * s(D)
        W_out = jax.random.normal(ks[7], (INNER, DIM), dtype=jnp.float32) * s(INNER)
        b_out = jnp.zeros((DIM,), dtype=jnp.float32)
        temperature = jnp.ones((1, H, 1, 1), dtype=jnp.float32) * 0.5
        return {'x': x, 'W_fx': W_fx, 'b_fx': b_fx, 'W_x': W_x, 'b_x': b_x, 'W_slice': W_slice, 'b_slice': b_slice, 'W_q': W_q, 'W_k': W_k, 'W_v': W_v, 'W_out': W_out, 'b_out': b_out, 'temperature': temperature}
    _L0_ffn_all = _L0_ffn_setup()
    _L0_ffn_in = {k: v for k, v in _L0_ffn_all.items() if k in ('W_fx', 'b_fx', 'W_x', 'b_x', 'W_slice', 'b_slice', 'W_q', 'W_k', 'W_v', 'W_out', 'b_out', 'temperature')}
    del _L0_ffn_all
    return {'x': x, 'src': src, 'dst': dst, 'L0_gnn_W0': _L0_gnn_in['W0'], 'L0_gnn_b0': _L0_gnn_in['b0'], 'L0_gnn_g0': _L0_gnn_in['g0'], 'L0_gnn_beta0': _L0_gnn_in['beta0'], 'L0_gnn_W1': _L0_gnn_in['W1'], 'L0_gnn_b1': _L0_gnn_in['b1'], 'L0_gnn_g1': _L0_gnn_in['g1'], 'L0_gnn_beta1': _L0_gnn_in['beta1'], 'L0_mix_w_qkv': _L0_mix_in['w_qkv'], 'L0_mix_bn_gamma': _L0_mix_in['bn_gamma'], 'L0_mix_bn_beta': _L0_mix_in['bn_beta'], 'L0_mix_w_dw': _L0_mix_in['w_dw'], 'L0_mix_w_pw': _L0_mix_in['w_pw'], 'L0_mix_w_res': _L0_mix_in['w_res'], 'L0_mix_b_res': _L0_mix_in['b_res'], 'L0_ffn_W_fx': _L0_ffn_in['W_fx'], 'L0_ffn_b_fx': _L0_ffn_in['b_fx'], 'L0_ffn_W_x': _L0_ffn_in['W_x'], 'L0_ffn_b_x': _L0_ffn_in['b_x'], 'L0_ffn_W_slice': _L0_ffn_in['W_slice'], 'L0_ffn_b_slice': _L0_ffn_in['b_slice'], 'L0_ffn_W_q': _L0_ffn_in['W_q'], 'L0_ffn_W_k': _L0_ffn_in['W_k'], 'L0_ffn_W_v': _L0_ffn_in['W_v'], 'L0_ffn_W_out': _L0_ffn_in['W_out'], 'L0_ffn_b_out': _L0_ffn_in['b_out'], 'L0_ffn_temperature': _L0_ffn_in['temperature']}

def reference(x, src, dst, L0_gnn_W0, L0_gnn_b0, L0_gnn_g0, L0_gnn_beta0, L0_gnn_W1, L0_gnn_b1, L0_gnn_g1, L0_gnn_beta1, L0_mix_w_qkv, L0_mix_bn_gamma, L0_mix_bn_beta, L0_mix_w_dw, L0_mix_w_pw, L0_mix_w_res, L0_mix_b_res, L0_ffn_W_fx, L0_ffn_b_fx, L0_ffn_W_x, L0_ffn_b_x, L0_ffn_W_slice, L0_ffn_b_slice, L0_ffn_W_q, L0_ffn_W_k, L0_ffn_W_v, L0_ffn_W_out, L0_ffn_b_out, L0_ffn_temperature):
    import jax
    import jax.numpy as jnp

    def _L0_gnn_ref(x, edge_index, W0, b0, g0, beta0, W1, b1, g1, beta1):
        import jax, jax.numpy as jnp
        import numpy as np
        N = 6250
        E = 200000
        D = 256
        H = 256
        EPS = 1e-05

        def _gnn_layer(x, row, col, W, b, g, beta):
            n = x.shape[0]
            neigh = x[col]
            agg = jax.ops.segment_sum(neigh, row, num_segments=n)
            deg = jax.ops.segment_sum(jnp.ones((row.shape[0],), x.dtype), row, num_segments=n)
            deg = jnp.maximum(deg, 1.0)[:, None]
            h = (x + agg / deg) @ W.T + b
            mu = jnp.mean(h, axis=-1, keepdims=True)
            var = jnp.mean(jnp.square(h - mu), axis=-1, keepdims=True)
            hn = (h - mu) * jax.lax.rsqrt(var + EPS) * g + beta
            return jax.nn.silu(hn)
        row, col = (edge_index[0], edge_index[1])
        x = _gnn_layer(x, row, col, W0, b0, g0, beta0)
        x = _gnn_layer(x, row, col, W1, b1, g1, beta1)
        return x

    def _L0_mix_ref(x, w_qkv, bn_gamma, bn_beta, w_dw, w_pw, w_res, b_res):
        import jax, jax.numpy as jnp
        import numpy as np
        C_CURV = 1.0
        MIN_NORM = 1e-15
        BALL_EPS = 1e-05
        ATT_EPS = 1e-15
        DIM = 32

        def _norm(x):
            return jnp.clip(jnp.linalg.norm(x, axis=-1, keepdims=True), MIN_NORM)

        def proj(x, c):
            maxnorm = (1.0 - BALL_EPS) / jnp.sqrt(c)
            n = _norm(x)
            return jnp.where(n > maxnorm, x / n * maxnorm, x)

        def expmap0(u, c):
            sc = jnp.sqrt(c)
            n = _norm(u)
            return jnp.tanh(sc * n) * u / (sc * n)

        def logmap0(p, c):
            sc = jnp.sqrt(c)
            n = _norm(p)
            return jnp.arctanh(jnp.clip(sc * n, -1.0 + 1e-07, 1.0 - 1e-07)) * p / (sc * n)

        def mobius_add(x, y, c):
            x2 = jnp.sum(x * x, -1, keepdims=True)
            y2 = jnp.sum(y * y, -1, keepdims=True)
            xy = jnp.sum(x * y, -1, keepdims=True)
            num = (1 + 2 * c * xy + c * y2) * x + (1 - c * x2) * y
            den = 1 + 2 * c * xy + c * c * x2 * y2
            return num / jnp.clip(den, MIN_NORM)

        def conv1d(x, w, pad, groups=1):
            return jax.lax.conv_general_dilated(x, w, (1,), [(pad, pad)], dimension_numbers=('NCH', 'OIH', 'NCH'), feature_group_count=groups)

        def batchnorm(x, gamma, beta):
            mean = jnp.mean(x, axis=(0, 2), keepdims=True)
            var = jnp.var(x, axis=(0, 2), keepdims=True)
            xn = (x - mean) * jax.lax.rsqrt(var + 1e-05)
            return gamma[None, :, None] * xn + beta[None, :, None]

        def _reference_tuple_inner(x, w_qkv, bn_gamma, bn_beta, w_dw, w_pw, w_res, b_res):
            c = C_CURV
            h = logmap0(proj(x, c), c)
            h = jnp.transpose(h, (1, 2, 0))
            h = conv1d(h, w_qkv, pad=2)
            h = batchnorm(h, bn_gamma, bn_beta)
            h = jax.nn.relu(jnp.transpose(h, (2, 0, 1)))
            qkv = proj(expmap0(h, c), c)
            t = jnp.transpose(logmap0(proj(qkv, c), c), (1, 2, 0))
            s = conv1d(t, w_dw, pad=2, groups=t.shape[1])
            s = conv1d(s, w_pw, pad=0, groups=t.shape[1] // DIM)
            cat = jnp.concatenate([t, s], axis=1)
            ai = proj(expmap0(jnp.transpose(cat, (2, 0, 1)), c), c)
            t2 = logmap0(proj(ai, c), c)
            L, N, C2 = t2.shape
            g = C2 // (3 * DIM)
            qkv3 = jnp.transpose(t2, (1, 2, 0)).reshape(N, g, 3 * DIM, L)
            q, k, v = jnp.split(qkv3, 3, axis=2)
            q = jax.nn.relu(q)
            k = jax.nn.relu(k)
            vk = jnp.einsum('ngdl,ngel->ngde', v, k)
            out = jnp.einsum('ngde,ngdl->ngdl', vk, q)
            out = out / (jnp.sum(v, -1, keepdims=True) + ATT_EPS)
            out = jnp.transpose(out.reshape(N, g * DIM, L), (2, 0, 1))
            fx_h = proj(expmap0(out, c), c)
            ft = jnp.transpose(logmap0(proj(fx_h, c), c), (1, 2, 0))
            ft = conv1d(ft, w_res, pad=0) + b_res[None, :, None]
            fx = proj(expmap0(jnp.transpose(ft, (2, 0, 1)), c), c)
            residual = mobius_add(fx, x, c)
            return (fx, residual)
        return _reference_tuple_inner(x, w_qkv, bn_gamma, bn_beta, w_dw, w_pw, w_res, b_res)[0]

    def _L0_ffn_ref(x, W_fx, b_fx, W_x, b_x, W_slice, b_slice, W_q, W_k, W_v, W_out, b_out, temperature):
        import jax, jax.numpy as jnp
        import numpy as np
        DIM = 256
        H = 8
        D = 64
        G = 64
        INNER = H * D
        SCALE = D ** (-0.5)
        B, N, _ = x.shape
        fx_mid = (x @ W_fx + b_fx).reshape(B, N, H, D).transpose(0, 2, 1, 3)
        x_mid = (x @ W_x + b_x).reshape(B, N, H, D).transpose(0, 2, 1, 3)
        temp = jnp.clip(temperature, 0.1, 5.0)
        slice_weights = jax.nn.softmax((x_mid @ W_slice + b_slice) / temp, axis=-1)
        slice_norm = slice_weights.sum(axis=2)
        slice_token = jnp.einsum('bhnc,bhng->bhgc', fx_mid, slice_weights)
        slice_token = slice_token / (slice_norm[..., None] + 1e-05)
        q = slice_token @ W_q
        k = slice_token @ W_k
        v = slice_token @ W_v
        attn = jax.nn.softmax(jnp.einsum('bhgc,bhkc->bhgk', q, k) * SCALE, axis=-1)
        out_slice = jnp.einsum('bhgk,bhkc->bhgc', attn, v)
        out_x = jnp.einsum('bhgc,bhng->bhnc', out_slice, slice_weights)
        out_x = out_x.transpose(0, 2, 1, 3).reshape(B, N, INNER)
        return out_x @ W_out + b_out
    edge_index = jnp.stack([src, dst])
    xn = _layernorm(x, axis=-1)
    x = x + _L0_gnn_ref(xn, edge_index, L0_gnn_W0, L0_gnn_b0, L0_gnn_g0, L0_gnn_beta0, L0_gnn_W1, L0_gnn_b1, L0_gnn_g1, L0_gnn_beta1) + _L0_mix_ref(xn[None], L0_mix_w_qkv, L0_mix_bn_gamma, L0_mix_bn_beta, L0_mix_w_dw, L0_mix_w_pw, L0_mix_w_res, L0_mix_b_res)[0]
    x = x + _L0_ffn_ref(_layernorm(x, axis=-1)[None], L0_ffn_W_fx, L0_ffn_b_fx, L0_ffn_W_x, L0_ffn_b_x, L0_ffn_W_slice, L0_ffn_b_slice, L0_ffn_W_q, L0_ffn_W_k, L0_ffn_W_v, L0_ffn_W_out, L0_ffn_b_out, L0_ffn_temperature)[0]
    return x

_drawn_inputs = setup_inputs


def setup_inputs(seed=0):
    import zlib

    import numpy as np

    out = dict(_drawn_inputs(seed))
    spreads = {'L0_gnn_g0': (1.0, 0.2),
     'L0_gnn_beta0': (0.0, 0.1),
     'L0_gnn_g1': (1.0, 0.2),
     'L0_gnn_beta1': (0.0, 0.1),
     'L0_mix_bn_gamma': (1.0, 0.6),
     'L0_mix_bn_beta': (0.0, 0.583),
     'L0_mix_b_res': (0.0, 0.361),
     'L0_ffn_b_fx': (0.0, 0.1),
     'L0_ffn_b_x': (0.0, 0.8),
     'L0_ffn_b_slice': (0.0, 0.8),
     'L0_ffn_b_out': (0.0, 0.1),
     'L0_ffn_temperature': (0.5, 0.6)}
    factors = {'L0_mix_w_dw': 8.0,
     'L0_mix_w_pw': 7.969,
     'L0_ffn_W_x': 7.896,
     'L0_ffn_W_slice': 8.0,
     'L0_ffn_W_q': 8.0,
     'L0_ffn_W_k': 8.0}
    for name, (base, spread) in spreads.items():
        noise = np.random.default_rng([zlib.crc32(name.encode()), seed]).standard_normal(out[name].shape)
        drawn = base * np.exp(spread * noise) if base else spread * noise
        out[name] = jnp.asarray(drawn.astype(out[name].dtype))
    for name, factor in factors.items():
        out[name] = (out[name] * factor).astype(out[name].dtype)
    return out
```

```python
import concourse.bass as bass
from concourse import mybir
from contextlib import ExitStack

F32 = mybir.dt.float32
BF16 = mybir.dt.bfloat16
I32 = mybir.dt.int32
U16 = mybir.dt.uint16
ALU = mybir.AluOpType
ACT = mybir.ActivationFunctionType
AX = mybir.AxisListType

N, D = 6250, 256
P = 128
PT, NT = 125, 50
E = 100000
EC = 782
EPAD = P * EC - E
NCH = 832
GRP = 8
NGRP = NCH // GRP
STG = 17
PIECE1 = 10
CH3 = 3 * D
NG = 16
H, HD, G = 8, 64, 64
HG = H * G
PADCODE = 1 << 20
LN_EPS = 1e-5
MAXN = 0.9999899864196777
ATANH_MAXN = 6.102372169494629


class Order:

    def __init__(self, eng, sem):
        self.eng, self.sem, self.total, self.base, self.local = eng, sem, 0, None, 0

    def value(self):
        return self.total if self.base is None else self.base + self.local

    def link(self, ins):
        ins.then_inc(self.sem, 1)
        if self.base is None:
            self.total += 1
        else:
            self.local += 1
        self.eng.wait_ge(self.sem, self.value())

    def enter(self, j, per_turn):
        self.base, self.local, self.per_turn = j * per_turn + self.total, 0, per_turn

    def leave(self, turns):
        assert self.local == self.per_turn, (self.local, self.per_turn)
        self.total += turns * self.per_turn
        self.base = None


def run_tiles(eng, order, step, n, lag):
    peel = lag + 2 + (lag % 2)
    for i in range(peel):
        before = order.total if order else 0
        step(i, i % 2)
    per = 2 * (order.total - before) if order else 0
    turns = (n - peel) // 2
    with eng.Fori(0, turns) as j:
        if order:
            order.enter(j, per)
        step(j * 2 + peel, 0)
        step(j * 2 + (peel + 1), 1)
        if order:
            order.leave(turns)
    for i in range(n, n + lag):
        step(i, i % 2)


def live(i, lag, n=NT):
    if isinstance(i, int):
        return i - lag if 0 <= i - lag < n else None
    return i - lag


def gps_kernel(nc, a, out):
    ctx = ExitStack()
    with ctx:
        def sb(name, shape, dt=F32):
            return ctx.enter_context(nc.sbuf_tensor(name, shape, dt))

        def sem(name):
            return ctx.enter_context(nc.semaphore(name))

        x_d = a["x"].rearrange("(p t) c -> p t c", t=NT)
        out_d = out.rearrange("(p t) c -> p t c", t=NT)
        table = [nc.dram_tensor(f"table{l}", (N, D), F32, kind="Internal").ap() for l in range(2)]
        table_d = [t.rearrange("(p t) c -> p t c", t=NT) for t in table]
        x2_dram = nc.dram_tensor("x2_rows", (N, D), F32, kind="Internal").ap()
        x2_d = x2_dram.rearrange("(p t) c -> p t c", t=NT)
        sorted_dram = nc.dram_tensor("sorted_edges", (P * NCH, 1), I32, kind="Internal").ap()
        sorted_rows = sorted_dram.rearrange("(p c) o -> p (c o)", p=P)

        nodes = sb("nodes", [PT, NT, D])
        big = sb("big", [P, NT * 257 + NT * D])
        acc = big[0:PT, 0:NT * 257].rearrange("p (t c) -> p t c", c=257)
        mixo = big[0:PT, NT * 257:].rearrange("p (t c) -> p t c", c=D)
        arena_a = sb("arena_a", [P, 4750])
        arena_b = sb("arena_b", [P, 16 * 257 + 2 * GRP * PT])

        def carve(arena, at, shape, dt=F32, parts=P):
            n = 1
            for s in shape:
                n *= s
            words = n if dt in (F32, I32) else (n + 1) // 2
            v = arena[0:parts, at:at + words]
            if dt != F32:
                v = v.bitcast(dt)
            if len(shape) == 2:
                v = v.rearrange("p (a b) -> p a b", b=shape[1])
            elif len(shape) == 3:
                v = v.rearrange("p (a b c) -> p a b c", b=shape[1], c=shape[2])
            return v, at + words

        e_src, o = carve(arena_a, 0, [EC], I32)
        code, o = carve(arena_a, o, [EC], I32)
        quot, o = carve(arena_a, o, [EC], I32)
        count_run = quot.bitcast(F32)
        pos_f, o = carve(arena_a, o, [EC])
        bin16, o = carve(arena_a, o, [EC], U16)
        mask16, o = carve(arena_a, o, [EC], U16)
        pos_i = e_src
        tile_row, o = carve(arena_a, o, [NCH], I32, 1)
        s_code, o = carve(arena_a, 0, [NCH], I32)
        s_dst, o = carve(arena_a, o, [NCH], I32)
        s_row, o = carve(arena_a, o, [NCH + 2 * GRP])
        fill, _ = carve(arena_b, 0, [NCH], I32)
        tcmp, _ = carve(arena_b, NCH, [NCH], F32, NT)
        triu, _ = carve(arena_b, 2 * NCH, [P])
        wstage, _ = carve(arena_b, 2 * NCH + P, [2, 2, D])
        gat, o = carve(arena_b, 0, [16, 257])
        onehot, o = carve(arena_b, o, [2 * GRP, PT])
        u_ring, o = carve(arena_b, 0, [2, D], F32, PT)
        uT_ring, o = carve(arena_b, o, [4, PT])
        gam, o = carve(arena_b, o, [D], F32, PT)
        bet, o = carve(arena_b, o, [D], F32, PT)
        z_ring, o = carve(arena_b, o, [2, D], F32, PT)
        pos_stage = sb("pos_stage", [P, 2, STG], I32)
        code_stage = sb("code_stage", [P, 2, STG], I32)
        dst_stage = sb("dst_stage", [P, 2, GRP], I32)

        ident = sb("ident", [P, P])
        ones = sb("ones", [P, P])
        iota_row = sb("iota_row", [P, PT])
        bin_id = sb("bin_id", [P, NT])
        counts = sb("counts", [P, NT])
        carry = sb("carry", [P, NT])
        bins = sb("bins", [P, 3, NT])
        bins_i = sb("bins_i", [P, NT], I32)
        chunk_end = sb("chunk_end", [NT, 1])
        ones3 = sb("ones3", [3, P], BF16)
        lnst = sb("lnst", [PT, NT, 6])
        mean = sb("mean", [PT, NT])
        cols = sb("cols", [PT, 4, NT])
        wT = [sb(f"w{l}T", [P, 2, D]) for l in range(2)]
        gbias3 = [sb(f"gbias3_{l}", [3, D], BF16) for l in range(2)]
        rT_ring, wa = carve(big, 0, [2, 6, PT])
        ev, wa = carve(big, wa, [4, NG * 32], F32, PT)
        junk, wa = carve(big, wa, [2, CH3], F32, PT)
        brow, wb = carve(big, 0, [2, D], F32, 3)
        split, wb = carve(big, wb, [4, CH3], F32, 3)
        split_bf, wb = carve(big, wb, [3, CH3], BF16, 3)
        assert wb <= wa
        wqkv, wa = carve(big, wa, [2, CH3])
        wqkv_flat = big[:, wa - 2 * CH3:wa]
        wblock, wa = carve(big, wa, [6, P])
        wres, wa = carve(big, wa, [4, D])
        wres_flat = big[:, wa - 4 * D:wa]
        bres, wa = carve(big, wa, [D], F32, PT)
        qbias3, wa = carve(big, wa, [CH3], BF16, 3)
        wres_stage, wa = carve(big, wa, [2, 2 * D])
        bn_gam, wa = carve(big, wa, [CH3])
        bn_bet, wa = carve(big, wa, [CH3])
        pw_stage, wa = carve(big, wa, [6, 32])
        pw_turned, wa = carve(big, wa, [6, 32])
        dw_stage, wa = carve(big, wa, [6, 5])
        hin, wa = carve(big, wa, [2, D], F32, PT)
        assert wa <= NT * 257
        xback = big[0:PT, 0:NT * D].rearrange("p (t c) -> p t c", c=D)
        wq_stage, wa = carve(big, NT * 257, [6, 5 * D])
        prod, wa = carve(big, wa, [4, CH3])
        cov, wa = carve(big, wa, [2, D])
        mu, wa = carve(big, wa, [D])
        muT, wa = carve(big, wa, [2])
        assert wa <= NT * 257 + NT * D
        cat, o = carve(arena_b, 0, [2, 2 * CH3], F32, PT)
        o_ring, o = carve(arena_b, o, [2, 2 * D], F32, PT)
        oT_ring, o = carve(arena_b, o, [8, PT])
        hT_ring, o = carve(arena_b, o, [4, PT])
        assert o <= 16 * 257 + 2 * GRP * PT
        ffw = big[0:PT, 0:NT * HG].rearrange("p (t c) -> p t c", c=HG)
        w_fx, o = carve(arena_a, 0, [2, HG])
        w_out, o = carve(arena_a, o, [H, D], F32, HD)
        wx_stage, o = carve(arena_a, o, [2, HG])
        beta_row = arena_a[0:1, o - 2 * HG:o - HG]
        b_fx, o = carve(arena_a, o, [HG], F32, 1)
        wc, o = carve(arena_b, 0, [2, HG])
        wxT_flat = arena_b[:, o:o + 4 * D]
        wxT, o = carve(arena_b, o, [4, D])
        xlT_ring, o = carve(arena_b, o, [4, PT])
        ex_ring, o = carve(arena_b, o, [2, HG], F32, PT)
        w_ring, o = carve(arena_b, o, [2, HG], F32, PT)
        xl_ring, o = carve(arena_b, o, [2, D], F32, PT)
        assert o <= 16 * 257 + 2 * GRP * PT
        wT_ring, o = carve(arena_b, 0, [8, PT])
        wcopy_ring, o = carve(arena_b, o, [2, HG], F32, PT)
        m_out, _ = carve(arena_b, 16 * 257 + 2 * GRP * PT - 4 * D, [4, D])
        tok, o = carve(arena_b, 0, [4, 257])
        tokT, o = carve(arena_b, o, [2, HG])
        osT = tokT.rearrange("p a b -> p (a b)")[0:HD, :].rearrange("p (h c) -> p h c", c=P)
        stok, o = carve(arena_b, o, [HG], F32, HD)
        attnT = stok
        qT, o = carve(arena_b, o, [HG], F32, HD)
        kT, o = carve(arena_b, o, [HG], F32, HD)
        vv, o = carve(arena_b, o, [HG], F32, HD)
        attn, o = carve(arena_b, o, [HG], F32, HD)
        assert o <= 16 * 257 + 2 * GRP * PT - 4 * D
        lbrow = brow.rearrange("p a b -> p (a b)")
        w_small = sb("w_small", [P, 4, HD])
        b_x8 = sb("b_x8", [H, HD])
        b_x8T = sb("b_x8T", [HD, H])
        b_sl = sb("b_sl", [3, G])
        inv_temp = sb("inv_temp", [P, H])
        lbias3 = sb("lbias3", [3, HG], BF16)
        head8 = sb("head8", [PT, 2, 3, H])
        fac = sb("fac", [PT, NT])
        nf2 = sb("nf2", [PT, NT])
        few = sb("few", [PT, NT], I32)
        sm = sb("sm", [PT, 2, 20])
        rb = sb("rb", [P, 2, 4])

        ps = ctx.enter_context(nc.psum_tensor("ps", [P, 8, 512], F32))

        sems = {}

        def s(name):
            if name not in sems:
                sems[name] = sem(name)
            return sems[name]

        block = ctx.enter_context(nc.Block())

        @block.sync
        def _(sp):
            sp.wait_ge(s("edges_padded"), 1)
            for src, dst in ((a["src"], e_src), (a["dst"], code)):
                full = (P - 1) * EC
                sp.dma_start(dst[0:P - 1, :], src[0:full].rearrange("(p c) -> p c", c=EC)).then_inc(s("edges_loaded"), 16)
                sp.dma_start(dst[P - 1:P, 0:EC - EPAD], src[full:E].rearrange("(p c) -> p c", p=1)).then_inc(s("edges_loaded"), 16)
            for k in range(5):
                sp.dma_start(nodes[:, 10 * k:10 * k + 10, :], x_d[:, 10 * k:10 * k + 10, :]).then_inc(s("x_loaded"), 16)
            sp.dma_start(wq_stage, a["L0_mix_w_qkv"].rearrange("(j p) c k -> p j (c k)", p=P)).then_inc(s("wq_loaded"), 16)
            sp.wait_ge(s("fill_set"), 1)
            sp.dma_start(sorted_rows, fill[:, :]).then_inc(s("sorted_cleared"), 16)
            sp.wait_ge(s("xn_ready"), 1)
            sp.dma_start(table_d[0], nodes[:, :, :]).then_inc(s("table0_stored"), 16)
            sp.wait_ge(s("mix_tiles_done"), 1)
            for k in range(5):
                sp.dma_start(xback[:, 10 * k:10 * k + 10, :], x_d[:, 10 * k:10 * k + 10, :]).then_inc(s("x_back"), 16)
            sp.wait_ge(s("scattered0"), 16 * STG * (EC // STG // 2))
            sp.wait_ge(s("scattered1"), 16 * STG * (EC // STG // 2))
            sp.dma_start(s_code, sorted_rows).then_inc(s("sorted_loaded"), 16)
            for l in range(2):
                sp.wait_ge(s("agg_added"), NCH * (l + 1))
                sp.dma_start(gam, a[f"L0_gnn_g{l}"].partition_broadcast(PT)).then_inc(s("gamma_loaded"), 16)
                sp.dma_start(bet, a[f"L0_gnn_beta{l}"].partition_broadcast(PT)).then_inc(s("gamma_loaded"), 16)
                if l == 0:
                    for k in range(5):
                        sp.wait_ge(s("silu_done"), 10 * (k + 1))
                        sp.dma_start(table_d[1][:, 10 * k:10 * k + 10, :], nodes[:, 10 * k:10 * k + 10, :]).then_inc(s("table1_stored"), 16)
            ffn = lambda name: a[f"L0_ffn_{name}"]
            for dst, src in ((w_fx, ffn("W_fx").rearrange("(k p) n -> p k n", p=P)),
                             (wx_stage, ffn("W_x").rearrange("(k p) n -> p k n", p=P)),
                             (w_out, ffn("W_out").rearrange("(h c) n -> c h n", c=HD)),
                             (b_fx, ffn("b_fx").rearrange("(o n) -> o n", o=1)),
                             (brow[:, 0, :], ffn("b_out").partition_broadcast(3))):
                if dst is w_fx:
                    sp.wait_ge(s("x2_ready"), 1)
                sp.dma_start(dst, src).then_inc(s("ffn_loaded"), 16)
            sp.dma_start(x2_d, nodes[:, :, :]).then_inc(s("x2_stored"), 16)
            sp.wait_ge(s("slices_summed"), 1)
            for k in range(5):
                sp.dma_start(nodes[:, 10 * k:10 * k + 10, :], x2_d[:, 10 * k:10 * k + 10, :]).then_inc(s("x2_back"), 16)
            for k in range(5):
                sp.wait_ge(s("out_ready"), 10 * (k + 1))
                sp.dma_start(out_d[:, 10 * k:10 * k + 10, :], nodes[:, 10 * k:10 * k + 10, :]).then_inc(s("out_stored"), 16)
            sp.wait_ge(s("out_stored"), 80)
            sp.wait_ge(s("table0_stored"), 16)
            sp.wait_ge(s("table1_stored"), 80)
            sp.wait_ge(s("x2_stored"), 16)

        @block.gpsimd
        def _(pool):
            po = Order(pool, s("pool_order"))
            iota = dict(base=0, channel_multiplier=0, allow_small_or_imprecise_dtypes=True)
            po.link(pool.memset(e_src[96:P, EC - EPAD:EC], 0))
            po.link(pool.memset(code[96:P, EC - EPAD:EC], PADCODE))
            pool.sem_inc(s("edges_padded"), 1)
            po.link(pool.iota(bin_id[:, :], [[1, NT]], **iota))
            pool.sem_inc(s("bin_id_set"), 1)
            po.link(pool.memset(fill[:, :], PADCODE))
            pool.sem_inc(s("fill_set"), 1)
            po.link(pool.memset(ones[:, :], 1.0))
            po.link(pool.memset(ones3[:, :], 1.0))
            po.link(pool.affine_select(out=triu[:, :], in_=ones[:, :], compare_op=ALU.is_gt, fill=0.0, base=0,
                                       pattern=[[1, P]], channel_multiplier=-1))
            po.link(pool.memset(ident[:, :], 0.0))
            po.link(pool.affine_select(out=ident[:, :], in_=ident[:, :], compare_op=ALU.not_equal, fill=1.0, base=0,
                                       pattern=[[-1, P]], channel_multiplier=1))
            po.link(pool.iota(iota_row[:, :], [[1, PT]], **iota))
            po.link(pool.iota(tcmp, [[1, NCH]], **iota))
            pool.sem_inc(s("consts_set"), 1)

            def scatter_batch(b, half, first):
                if not first:
                    pool.wait_ge(s(f"scattered{half}"), b[0] * (16 * STG))
                c0 = (b[0] * 2 + half) * STG
                pool.tensor_copy(pos_stage[:, half, :], pos_i[:, bass.ds(c0, STG)]).then_inc(s("staged"), 1)
                pool.wait_ge(s("staged"), (b[0] * 2 + half) * 2 + 1)
                pool.nop(nofuse=True)
                pool.tensor_copy(code_stage[:, half, :], code[:, bass.ds(c0, STG)]).then_inc(s("staged"), 1)
                pool.wait_ge(s("staged"), (b[0] * 2 + half) * 2 + 2)
                pool.nop(nofuse=True)
                for k in range(STG):
                    pool.indirect_dma_start(
                        sorted_dram, bass.IndirectOffsetOnAxis(ap=pos_stage[:, half, k:k + 1], axis=0),
                        code_stage[:, half, k:k + 1], None).then_inc(s(f"scattered{half}"), 16)

            pool.wait_ge(s("positions"), 1)
            pool.wait_ge(s("sorted_cleared"), 16)
            for half in range(2):
                scatter_batch([0], half, True)
            with pool.Fori(1, PIECE1 // 2) as j:
                for half in range(2):
                    scatter_batch([j], half, False)
            pool.wait_ge(s("positions"), 2)
            with pool.Fori(PIECE1 // 2, EC // STG // 2) as j:
                for half in range(2):
                    scatter_batch([j], half, False)

            def gather_group(l, j, half, first):
                if not first:
                    pool.wait_ge(s("agg_made"), (j * 2 + half) * GRP + (NCH * l - GRP))
                pool.tensor_copy(dst_stage[:, half, :], s_dst[:, bass.ds((j * 2 + half) * GRP, GRP)]).then_inc(s("dst_staged"), 1)
                pool.wait_ge(s("dst_staged"), (j * 2 + half) + (NGRP * l + 1))
                pool.nop(nofuse=True)
                for k in range(GRP):
                    pool.indirect_dma_start(
                        gat[:, GRP * half + k, 0:D], None, table[l],
                        bass.IndirectOffsetOnAxis(ap=dst_stage[:, half, k:k + 1], axis=0)).then_inc(s(f"gathered{half}"), 16)

            for l in range(2):
                if l == 0:
                    pool.wait_ge(s("sorted_split"), 1)
                    pool.wait_ge(s("ring_free"), 1)
                    pool.wait_ge(s("table0_stored"), 16)
                else:
                    pool.wait_ge(s("ring_free"), 2)
                    pool.wait_ge(s("table1_stored"), 80)
                for half in range(2):
                    gather_group(l, 0, half, True)
                with pool.Fori(1, NGRP // 2) as j:
                    for half in range(2):
                        gather_group(l, j, half, False)

            def slice_step(i, par):
                t = live(i, 0)
                if t is not None:
                    pool.wait_ge(s("xl_ready"), t + 1)
                    pool.nop(nofuse=True)
                    po.link(pool.tensor_copy(nodes[:, bass.ds(t, 1), :], xl_ring[:, par:par + 1, :]))
                    pool.sem_inc(s("xl_copied"), 1)
                t = live(i, 2)
                if t is not None:
                    pool.wait_ge(s("w_ready"), t + 1)
                    pool.nop(nofuse=True)
                    po.link(pool.tensor_copy(ffw[:, bass.ds(t, 1), :], w_ring[:, par:par + 1, :]))
                    pool.sem_inc(s("w_kept"), 1)
            run_tiles(pool, po, slice_step, NT, 2)

            pool.wait_ge(s("slices_summed"), 1)
            pool.wait_ge(s("m_made"), 1)

            def out_step(i, par):
                t = live(i, 0)
                if t is not None:
                    if not isinstance(t, int) or t >= 2:
                        pool.wait_ge(s("w_turned"), t - 1)
                        pool.nop(nofuse=True)
                    po.link(pool.tensor_copy(wcopy_ring[:, par:par + 1, :], ffw[:, bass.ds(t, 1), :]))
                    pool.sem_inc(s("w_copied_back"), 1)
            run_tiles(pool, po, out_step, NT, 0)

        @block.scalar
        def _(act):
            ao = Order(act, s("act_order"))
            for l in range(2):
                act.dma_start(wstage[:, l, :, :], a[f"L0_gnn_W{l}"].rearrange("(b p) d -> p b d", p=P)).then_inc(s("gw_loaded"), 16)
                act.dma_start(brow[:, l, :], a[f"L0_gnn_b{l}"].partition_broadcast(3)).then_inc(s("gw_loaded"), 16)
            mix = lambda name: a[f"L0_mix_{name}"]
            ffn = lambda name: a[f"L0_ffn_{name}"]
            for dst, src in ((wres_stage, mix("w_res").rearrange("(b p) c k -> p b (c k)", p=P)),
                             (pw_stage, mix("w_pw").rearrange("(j p) c k -> p j (c k)", p=P)),
                             (dw_stage, mix("w_dw").rearrange("(j p) c k -> p j (c k)", p=P)),
                             (bn_gam, mix("bn_gamma").partition_broadcast(P)),
                             (bn_bet, mix("bn_beta").partition_broadcast(P)),
                             (bres, mix("b_res").partition_broadcast(PT)),
                             (w_small[0:HD, 0, :], ffn("W_slice")),
                             (w_small[HD:P, 0, :], ffn("W_slice")),
                             (w_small[0:HD, 1, :], ffn("W_q")),
                             (w_small[0:HD, 2, :], ffn("W_k")),
                             (w_small[0:HD, 3, :], ffn("W_v")),
                             (b_x8[:, :], ffn("b_x").rearrange("(h c) -> h c", c=HD)),
                             (b_sl[:, :], ffn("b_slice").partition_broadcast(3)),
                             (inv_temp[:, :], ffn("temperature").rearrange("a h b c -> (a h b c)").partition_broadcast(P))):
                act.dma_start(dst, src).then_inc(s("small_loaded"), 16)
            for l in range(2):
                act.wait_ge(s("gw_turned"), l + 1)
                for k in range(2):
                    act.activation(wT[l][:, k, :], ps[:, 4 + l, k * D:(k + 1) * D], ACT.Copy).then_inc(s("gw_ready"), 1)
            for b in range(5):
                act.wait_ge(s("mw_turned"), b + 1)
                dst = wqkv_flat[:, b * 512:(b + 1) * 512] if b < 3 else wres_flat[:, (b - 3) * 512:(b - 2) * 512]
                act.activation(dst, ps[:, b, :], ACT.Copy).then_inc(s("mw_ready"), 1)
            act.wait_ge(s("xvar_ready"), 1)
            act.activation(cols[:, 1, :], cols[:, 0, :], ACT.Sqrt).then_inc(s("xstd_ready"), 1)

            act.wait_ge(s("xnorm2_ready"), 1)
            act.activation(cols[:, 1, :], cols[:, 0, :], ACT.Sqrt).then_inc(s("xnorm_ready"), 1)
            act.wait_ge(s("log_args"), 1)
            act.activation(cols[:, 0, :], cols[:, 0, :], ACT.Ln).then_inc(s("logs_ready"), 1)
            act.activation(cols[:, 3, :], cols[:, 3, :], ACT.Ln).then_inc(s("logs_ready"), 1)
            act.wait_ge(s("means_summed"), 1)
            act.activation(mu, ps[:, 0, 0:D], ACT.Copy, scale=1.0 / N).then_inc(s("mu_ready"), 1)
            act.wait_ge(s("mu_turned"), 1)
            act.activation(muT.unsqueeze(2), ps[:, 3, 0:2 * P].rearrange("p (k c) -> p k c", k=2)[:, :, 0:1], ACT.Copy).then_inc(s("muT_ready"), 1)
            act.wait_ge(s("gram_made"), 1)
            act.activation(cov, ps[:, 1:3, 0:D], ACT.Copy, scale=1.0 / N).then_inc(s("cov_ready"), 1)
            act.wait_ge(s("bnvar_ready"), 1)
            act.activation(prod[:, 1, :], prod[:, 0, :], ACT.Sqrt).then_inc(s("bnstd_ready"), 1)

            act.wait_ge(s("sorted_cleared"), 16)

            def mix_step(i, par):
                q = 1 - par
                t = live(i, 0)
                if t is not None:
                    act.wait_ge(s("hin_turned"), t + 1)
                    if not isinstance(t, int) or t >= 2:
                        act.wait_ge(s("qkv_made"), t - 1)
                    act.activation(hT_ring[:, 2 * par:2 * par + 2, :], ps[:, 6, 0:2 * PT].rearrange("p (k c) -> p k c", k=2), ACT.Copy).then_inc(s("hT_ready"), 1)
                t = live(i, 1)
                if t is not None:
                    act.wait_ge(s("r_turned"), t + 1)
                    if not isinstance(t, int) or t >= 2:
                        act.wait_ge(s("s_made"), t - 1)
                    act.activation(rT_ring[:, q, :, :].rearrange("p (a b) c -> p a (b c)", a=2), ps[:, 4:6, 0:3 * PT], ACT.Copy).then_inc(s("rT_ready"), 1)
                t = live(i, 2)
                if t is not None:
                    act.wait_ge(s("o_turned"), t + 1)
                    if not isinstance(t, int) or t >= 2:
                        act.wait_ge(s("ft_made"), t - 1)
                    act.activation(oT_ring[:, 4 * par:4 * par + 4, :], ps[:, 7, 0:4 * PT].rearrange("p (k c) -> p k c", k=4), ACT.Copy).then_inc(s("oT_ready"), 1)
                    ao.link(act.activation(junk[:, 0, 0:2 * D], o_ring[:, par, :], ACT.Square, accum_out=sm[:, par, 3:4]))
                    act.sem_inc(s("on2_ready"), 1)
                t = live(i, 0)
                if t is not None:
                    act.wait_ge(s("qkv_made"), t + 1)
                    if not isinstance(t, int) or t >= 2:
                        act.wait_ge(s("o_ready"), t - 1)
                    ao.link(act.activation(cat[:, par, 0:CH3].rearrange("p (a b) -> p a b", a=2), ps[0:PT, 0:2, 0:CH3 // 2], ACT.Relu))
                    act.sem_inc(s("relu_done"), 1)
                    ao.link(act.activation(junk[:, 0, :], cat[:, par, 0:CH3], ACT.Square, accum_out=sm[:, par, 0:1]))
                t = live(i, 2)
                if t is not None:
                    act.wait_ge(s("on2_clipped"), t + 1)
                    act.activation(sm[:, par, 15:16], sm[:, par, 15:16], ACT.Sqrt).then_inc(s("on_ready"), 1)
                t = live(i, 1)
                if t is not None:
                    act.wait_ge(s("s_made"), t + 1)
                    ao.link(act.activation(cat[:, q, CH3:].rearrange("p (a b) -> p a b", a=2), ps[0:PT, 2:4, 0:CH3 // 2], ACT.Copy))
                    act.sem_inc(s("s_kept"), 1)
                    ao.link(act.activation(junk[:, 1, :], cat[:, q, CH3:], ACT.Square, accum_out=sm[:, q, 1:2]))
                    act.sem_inc(s("norms2_ready"), 1)
                    act.wait_ge(s("norms2_clipped"), t + 1)
                    act.activation(sm[:, q, 5:7], sm[:, q, 5:7], ACT.Sqrt).then_inc(s("norms_ready"), 1)
                t = live(i, 2)
                if t is not None:
                    act.wait_ge(s("ft_kept"), t + 1)
                    ao.link(act.activation(junk[:, 1, 0:D].unsqueeze(1), mixo[:, bass.ds(t, 1), :], ACT.Square, accum_out=nf2[:, bass.ds(t, 1)]))
            run_tiles(act, ao, mix_step, NT, 2)
            act.sem_inc(s("mix_tiles_done"), 1)
            act.wait_ge(s("fnorm2_ready"), 1)
            ao.link(act.activation(cols[:, 1, :], cols[:, 0, :], ACT.Sqrt))
            act.activation(cols[:, 2, :], cols[:, 1, :], ACT.Tanh).then_inc(s("ftanh_ready"), 1)

            for l in range(2):
                def post_step(i, par, l=l):
                    t = live(i, 0)
                    if t is not None:
                        act.wait_ge(s("u_turned"), t + (NT * l + 1))
                        if not isinstance(t, int) or t >= 2:
                            act.wait_ge(s("h_made"), t + (NT * l - 1))
                        act.activation(uT_ring[:, 2 * par:2 * par + 2, :],
                                       ps[:, 4 + par, 0:D].rearrange("p (k c) -> p k c", k=2)[:, :, 0:PT],
                                       ACT.Copy).then_inc(s("uT_ready"), 1)
                    t = live(i, 1)
                    if t is not None:
                        act.wait_ge(s("h_made"), t + (NT * l + 1))
                        act.activation(acc[:, bass.ds(t, 1), 0:D], ps[0:PT, 6 + 1 - par, 0:D].unsqueeze(1),
                                       ACT.Copy).then_inc(s("h_kept"), 1)
                run_tiles(act, None, post_step, NT, 1)
                act.wait_ge(s("hvar_ready"), l + 1)
                act.activation(cols[:, 1, :], cols[:, 0, :], ACT.Sqrt).then_inc(s("hstd_ready"), 1)
                with act.Fori(0, NT) as t:
                    act.wait_ge(s("z_ready"), t + (NT * l + 1))
                    dst = nodes[:, bass.ds(t, 1), :] if l == 0 else acc[:, bass.ds(t, 1), 0:D]
                    act.activation(dst, acc[:, bass.ds(t, 1), 0:D], ACT.Silu).then_inc(s("silu_done"), 1)

            for b in range(2):
                act.wait_ge(s("wx_turned"), b + 1)
                act.activation(wxT_flat[:, b * 512:(b + 1) * 512], ps[:, b, :], ACT.Copy).then_inc(s("wxT_ready"), 1)
            act.wait_ge(s("bx_turned"), 1)
            act.activation(b_x8T[:, :], ps[0:HD, 2, 0:H], ACT.Copy).then_inc(s("bxT_ready"), 1)
            act.wait_ge(s("yvar_ready"), 1)
            act.activation(cols[:, 1, :], cols[:, 0, :], ACT.Sqrt).then_inc(s("ystd_ready"), 1)

            def slice_step(i, par):
                t = live(i, 0)
                if t is not None:
                    act.wait_ge(s("xl_turned"), t + 1)
                    if not isinstance(t, int) or t >= 2:
                        act.wait_ge(s("logits_made"), t - 1)
                    act.activation(xlT_ring[:, 2 * par:2 * par + 2, :], ps[:, 6 + par, 0:2 * PT].rearrange("p (k c) -> p k c", k=2), ACT.Copy).then_inc(s("xlT_ready"), 1)
                t = live(i, 1)
                if t is not None:
                    q = 1 - par
                    act.wait_ge(s("shifted"), t + 1)
                    act.activation(ex_ring[:, q, :], ex_ring[:, q, :], ACT.Exp).then_inc(s("exp_done"), 1)
            run_tiles(act, None, slice_step, NT, 1)

            act.wait_ge(s("tok_turned"), 1)
            act.activation(tokT, ps[:, 4:6, :], ACT.Copy).then_inc(s("tokT_ready"), 1)
            act.activation(beta_row, ps[0:1, 6, :], ACT.Copy).then_inc(s("tokT_ready"), 1)
            act.wait_ge(s("stok_made"), 1)
            act.activation(stok, ps[0:HD, 0, :], ACT.Copy).then_inc(s("stok_ready"), 1)
            act.wait_ge(s("qkv_slices_made"), 1)
            for k, dst in enumerate((qT, kT, vv)):
                act.activation(dst, ps[0:HD, 1 + k, :], ACT.Copy).then_inc(s("qkv_slices_ready"), 1)
            act.wait_ge(s("scores_shifted"), 1)
            act.activation(attn, attn, ACT.Exp, scale=HD ** -0.5).then_inc(s("scores_exp"), 1)
            act.wait_ge(s("attn_turned"), 1)
            act.activation(attnT, ps[0:HD, 5, :], ACT.Copy).then_inc(s("attnT_ready"), 1)
            act.wait_ge(s("os_made"), 1)
            act.wait_ge(s("osT_zeroed"), 1)
            for hh in range(2):
                act.activation(osT[:, hh:H:2, hh * HD:(hh + 1) * HD],
                               ps[0:HD, 6, :].rearrange("p (h c) -> p h c", c=HD)[:, hh:H:2, :], ACT.Copy).then_inc(s("osT_ready"), 1)
            act.wait_ge(s("m_made"), 1)
            act.activation(m_out, ps[:, 0:4, 0:D], ACT.Copy).then_inc(s("m_ready"), 1)

            def out_step(i, par):
                t = live(i, 0)
                if t is not None:
                    act.wait_ge(s("w_turned"), t + 1)
                    if not isinstance(t, int) or t >= 2:
                        act.wait_ge(s("y_made"), t - 1)
                    act.activation(wT_ring[:, 4 * par:4 * par + 4, :], ps[:, par, 0:4 * PT].rearrange("p (k c) -> p k c", k=4), ACT.Copy).then_inc(s("wT_ready"), 1)
            run_tiles(act, None, out_step, NT, 0)

        @block.tensor
        def _(pe):
            pe.wait_ge(s("consts_set"), 1)
            pe.wait_ge(s("gw_loaded"), 64)
            for l in range(2):
                for k in range(2):
                    for b in range(2):
                        mm = pe.transpose(ps[:, 4 + l, k * D + b * P:k * D + (b + 1) * P],
                                          wstage[:, l, b, k * P:(k + 1) * P], ident[:, :])
                mm.then_inc(s("gw_turned"), 1)
            pe.wait_ge(s("wq_loaded"), 16)
            pe.wait_ge(s("small_loaded"), 14 * 16)
            for n in range(12):
                k, j = divmod(n, 6)
                taps = wq_stage[:, j, :].rearrange("p (c f) -> p c f", f=5)
                mm = pe.transpose(ps[:, n // 4, n % 4 * P:(n % 4 + 1) * P], taps[:, k * P:(k + 1) * P, 2], ident[:, :])
                if n % 4 == 3:
                    mm.then_inc(s("mw_turned"), 1)
            for n in range(8):
                k, b = divmod(n, 2)
                if n == 4:
                    pe.wait_ge(s("gw_ready"), 4)
                mm = pe.transpose(ps[:, 3 + n // 4, n % 4 * P:(n % 4 + 1) * P], wres_stage[:, b, k * P:(k + 1) * P], ident[:, :])
                if n % 4 == 3:
                    mm.then_inc(s("mw_turned"), 1)
            pe.wait_ge(s("counts_ready"), 1)
            pe.matmul(ps[:, 7, 0:NT], triu[:, :], counts[:, :], start=True, stop=True)
            pe.matmul(ps[:, 7, 64:64 + NT], ones[:, :], counts[:, :], start=True, stop=True).then_inc(s("totals_made"), 1)
            pe.wait_ge(s("ends_ready"), 1)
            pe.transpose(ps[0:NT, 6, 0:P], bins[:, 1, :], ident[:, :]).then_inc(s("ends_turned"), 1)
            pe.wait_ge(s("tcmp_ready"), 1)
            half = NCH // 2
            for k in range(2):
                mm = pe.matmul(ps[0:1, 6 + k, 0:half], ones[0:NT, 0:1], tcmp[:, k * half:(k + 1) * half], start=True, stop=True)
            mm.then_inc(s("tiles_made"), 1)

            pe.wait_ge(s("mw_ready"), 5)
            def mean_step(i, par):
                t = live(i, 1)
                if t is not None:
                    pe.wait_ge(s("scaled"), t + 1)
                    pe.matmul(ps[:, 0, 0:D], ones[0:PT, :], hin[:, 1 - par, :], start=isinstance(t, int) and t == 0,
                              stop=isinstance(t, int) and t == NT - 1).then_inc(s("scaled_used"), 1)
            run_tiles(pe, None, mean_step, NT, 1)
            pe.wait_ge(s("scaled_used"), NT)
            pe.sem_inc(s("means_summed"), 1)
            pe.wait_ge(s("mu_ready"), 1)
            for k in range(2):
                mm = pe.transpose(ps[:, 3, k * P:(k + 1) * P], mu[:, k * P:(k + 1) * P], ident[:, :])
            mm.then_inc(s("mu_turned"), 1)

            def gram_step(i, par):
                t = live(i, 1)
                if t is not None:
                    q = 1 - par
                    pe.wait_ge(s("centred"), t + 1)
                    first, last = isinstance(t, int) and t == 0, isinstance(t, int) and t == NT - 1
                    for k in range(2):
                        mm = pe.matmul(ps[:, 1 + k, 0:D], hin[:, q, k * P:(k + 1) * P], hin[:, q, :], start=first, stop=last)
                    mm.then_inc(s("centred_used"), 1)
            run_tiles(pe, None, gram_step, NT, 1)
            pe.wait_ge(s("centred_used"), NT)
            pe.sem_inc(s("gram_made"), 1)
            pe.wait_ge(s("cov_ready"), 1)
            pe.wait_ge(s("tiles_kept"), 1)
            for m in range(2):
                for n in range(2):
                    for k in range(2):
                        mm = pe.matmul(ps[:, 4 + 2 * m + n, 0:CH3 // 2], cov[:, k, m * P:(m + 1) * P],
                                       wqkv[:, k, n * CH3 // 2:(n + 1) * CH3 // 2], start=(k == 0), stop=(k == 1))
            mm.then_inc(s("cw_made"), 1)
            pe.wait_ge(s("prods_ready"), 1)
            for w in range(2):
                for n in range(2):
                    for k in range(2):
                        mm = pe.matmul(ps[:, 2 * w + n, 0:CH3 // 2], ones[:, :], prod[:, 2 * w + k, n * CH3 // 2:(n + 1) * CH3 // 2],
                                       start=(k == 0), stop=(k == 1))
            mm.then_inc(s("bnsums_made"), 1)

            pe.wait_ge(s("mixw_ready"), 1)

            def mix_step(i, par):
                q = 1 - par
                t = live(i, 0)
                if t is not None:
                    pe.wait_ge(s("hin_ready"), t + 1)
                    if not isinstance(t, int) or t >= 3:
                        pe.wait_ge(s("ft_kept"), t - 2)
                    if not (isinstance(t, int) and t == 0):
                        pe.wait_ge(s("hT_ready"), t)
                    for k in range(2):
                        mm = pe.transpose(ps[:, 6, k * PT:(k + 1) * PT], hin[:, par, k * P:(k + 1) * P], ident[0:PT, 0:PT])
                    mm.then_inc(s("hin_turned"), 1)
                t = live(i, 1)
                if t is not None:
                    pe.wait_ge(s("relu_done"), t + 1)
                    if not (isinstance(t, int) and t == 0):
                        pe.wait_ge(s("rT_ready"), t)
                    for j in range(6):
                        mm = pe.transpose(ps[:, 4 + j // 3, j % 3 * PT:(j % 3 + 1) * PT], cat[:, q, j * P:(j + 1) * P], ident[0:PT, 0:PT])
                    mm.then_inc(s("r_turned"), 1)
                t = live(i, 2)
                if t is not None:
                    pe.wait_ge(s("o_ready"), t + 1)
                    if not (isinstance(t, int) and t == 0):
                        pe.wait_ge(s("oT_ready"), t)
                    for j in range(4):
                        mm = pe.transpose(ps[:, 7, j * PT:(j + 1) * PT], o_ring[:, par, j * P:(j + 1) * P], ident[0:PT, 0:PT])
                    mm.then_inc(s("o_turned"), 1)
                t = live(i, 0)
                if t is not None:
                    pe.wait_ge(s("hT_ready"), t + 1)
                    if not (isinstance(t, int) and t == 0):
                        pe.wait_ge(s("relu_done"), t)
                    for n in range(2):
                        cs = slice(n * CH3 // 2, (n + 1) * CH3 // 2)
                        pe.matmul(ps[0:PT, n, 0:CH3 // 2], ones3[:, 0:PT], qbias3[:, cs], start=True, stop=False)
                        for k in range(2):
                            mm = pe.matmul(ps[0:PT, n, 0:CH3 // 2], hT_ring[:, 2 * par + k, :], wqkv[:, k, cs], start=False, stop=(k == 1))
                    mm.then_inc(s("qkv_made"), 1)
                t = live(i, 1)
                if t is not None:
                    pe.wait_ge(s("rT_ready"), t + 1)
                    if not (isinstance(t, int) and t == 0):
                        pe.wait_ge(s("s_kept"), t)
                    for j in range(6):
                        mm = pe.matmul(ps[0:PT, 2 + j // 3, j % 3 * P:(j % 3 + 1) * P], rT_ring[:, q, j, :], wblock[:, j, :], start=True, stop=True)
                    mm.then_inc(s("s_made"), 1)
                t = live(i, 2)
                if t is not None:
                    pe.wait_ge(s("oT_ready"), t + 1)
                    for j in range(4):
                        mm = pe.matmul(ps[0:PT, 6, D:2 * D], oT_ring[:, 4 * par + j, :], wres[:, j, :], start=(j == 0), stop=(j == 3))
                    mm.then_inc(s("ft_made"), 1)
            run_tiles(pe, None, mix_step, NT, 2)

            for l in range(2):
                pe.wait_ge(s("agg_added_credit"), 1)

                def group(j, half, l=l):
                    pe.wait_ge(s("onehot_ready"), (j * 2 + half) + (NGRP * l + 1))
                    pe.wait_ge(s(f"gathered{half}"), (j + (NGRP // 2 * l + 1)) * (16 * GRP))
                    for k in range(GRP):
                        n = (j * 2 + half) * GRP + (k + NCH * l)
                        if not (isinstance(n, int) and n < 4):
                            pe.wait_ge(s("agg_added"), n - 3)
                        pe.matmul(ps[0:PT, k % 4, 0:257], onehot[:, GRP * half + k, :], gat[:, GRP * half + k, :],
                                  start=True, stop=True).then_inc(s("agg_made"), 1)
                for half in range(2):
                    group(0, half)
                with pe.Fori(1, NGRP // 2) as j:
                    for half in range(2):
                        group(j, half)

                def post_step(i, par, l=l):
                    t = live(i, 0)
                    if t is not None:
                        pe.wait_ge(s("u_ready"), t + (NT * l + 1))
                        if not isinstance(t, int) or t >= 2:
                            pe.wait_ge(s("uT_ready"), t + (NT * l - 1))
                        for k in range(2):
                            mm = pe.transpose(ps[:, 4 + par, k * P:k * P + PT], u_ring[:, par, k * P:(k + 1) * P], ident[0:PT, 0:PT])
                        mm.then_inc(s("u_turned"), 1)
                    t = live(i, 1)
                    if t is not None:
                        q = 1 - par
                        pe.wait_ge(s("uT_ready"), t + (NT * l + 1))
                        if not isinstance(t, int) or t >= 2:
                            pe.wait_ge(s("h_kept"), t + (NT * l - 1))
                        pe.matmul(ps[0:PT, 6 + q, 0:D], ones3[:, 0:PT], gbias3[l][:, :], start=True, stop=False)
                        for k in range(2):
                            mm = pe.matmul(ps[0:PT, 6 + q, 0:D], uT_ring[:, 2 * q + k, :], wT[l][:, k, :],
                                           start=False, stop=(k == 1))
                        mm.then_inc(s("h_made"), 1)
                pe.wait_ge(s("gw_ready"), 4)
                pe.wait_ge(s("gbias_ready"), 2)
                run_tiles(pe, None, post_step, NT, 1)

            pe.wait_ge(s("ffn_loaded"), 80)
            for n in range(8):
                j, k = divmod(n, 2)
                mm = pe.transpose(ps[:, n // 4, n % 4 * P:(n % 4 + 1) * P], wx_stage[:, k, j * P:(j + 1) * P], ident[:, :])
                if n % 4 == 3:
                    mm.then_inc(s("wx_turned"), 1)
            pe.transpose(ps[0:HD, 2, 0:H], b_x8[:, :], ident[0:H, 0:H]).then_inc(s("bx_turned"), 1)
            pe.wait_ge(s("wxT_ready"), 2)
            for k in range(2):
                for h in range(H):
                    r0 = h % 2 * HD
                    mm = pe.matmul(ps[:, 4 + 2 * (h % 2) + k, h * G:(h + 1) * G], wxT[r0:r0 + HD, h // 2, k * P:(k + 1) * P],
                                   w_small[r0:r0 + HD, 0, :], start=True, stop=True)
            mm.then_inc(s("wc_made"), 1)
            pe.wait_ge(s("bxT_ready"), 1)
            for h in range(H):
                mm = pe.matmul(ps[0:3, 3, h * G:(h + 1) * G], b_x8T[:, h:h + 1].to_broadcast([HD, 3]), w_small[0:HD, 0, :], start=True, stop=True)
            mm.then_inc(s("lb_made"), 1)

            pe.wait_ge(s("wc_ready"), 1)

            def slice_step(i, par):
                t = live(i, 0)
                if t is not None:
                    pe.wait_ge(s("xl_ready"), t + 1)
                    if not isinstance(t, int) or t >= 2:
                        pe.wait_ge(s("xlT_ready"), t - 1)
                    for k in range(2):
                        mm = pe.transpose(ps[:, 6 + par, k * PT:(k + 1) * PT], xl_ring[:, par, k * P:(k + 1) * P], ident[0:PT, 0:PT])
                    mm.then_inc(s("xl_turned"), 1)
                t = live(i, 1)
                if t is not None:
                    q = 1 - par
                    pe.wait_ge(s("xlT_ready"), t + 1)
                    if not isinstance(t, int) or t >= 2:
                        pe.wait_ge(s("shifted"), t - 1)
                    pe.matmul(ps[0:PT, 4 + q, :], ones3[:, 0:PT], lbias3[:, :], start=True, stop=False)
                    for k in range(2):
                        mm = pe.matmul(ps[0:PT, 4 + q, :], xlT_ring[:, 2 * q + k, :], wc[:, k, :], start=False, stop=(k == 1))
                    mm.then_inc(s("logits_made"), 1)
                t = live(i, 3)
                if t is not None:
                    pe.wait_ge(s("w_ready"), t + 1)
                    pe.wait_ge(s("xl_copied"), t + 1)
                    first, last = isinstance(t, int) and t == 0, isinstance(t, int) and t == NT - 1
                    for j in range(4):
                        w = w_ring[:, 1 - par, j * P:(j + 1) * P]
                        pe.matmul(ps[:, j, 0:D], w, nodes[:, bass.ds(t, 1), :].squeeze(), start=first, stop=last, skip_group_check=True)
                        mm = pe.matmul(ps[:, j, D:D + 1], w, ones[0:PT, 0:1], start=False, stop=last, skip_group_check=True)
                    mm.then_inc(s("w_used"), 1)
            run_tiles(pe, None, slice_step, NT, 3)
            pe.wait_ge(s("w_used"), NT)
            pe.sem_inc(s("slices_summed"), 1)

            pe.wait_ge(s("tok_ready"), 1)
            for k in range(2):
                for j in range(4):
                    pe.transpose(ps[:, 4 + k, j * P:(j + 1) * P], tok[:, j, k * P:(k + 1) * P], ident[:, :])
            for j in range(4):
                mm = pe.transpose(ps[0:1, 6, j * P:(j + 1) * P], tok[:, j, D:D + 1], ident[:, :])
            mm.then_inc(s("tok_turned"), 1)
            pe.wait_ge(s("tokT_ready"), 2)
            for h in range(H):
                hs = slice(h * HD, (h + 1) * HD)
                for k in range(2):
                    pe.matmul(ps[0:HD, 0, hs], w_fx[:, k, hs], tokT[:, k, hs], start=(k == 0), stop=False)
                mm = pe.matmul(ps[0:HD, 0, hs], b_fx[:, hs], beta_row[:, hs], start=False, stop=True)
            mm.then_inc(s("stok_made"), 1)
            pe.wait_ge(s("stok_ready"), 1)
            pe.matmul(ps[0:HD, 1, :], w_small[0:HD, 1, :], stok, start=True, stop=True)
            pe.matmul(ps[0:HD, 2, :], w_small[0:HD, 2, :], stok, start=True, stop=True)
            for h in range(H):
                hs = slice(h * HD, (h + 1) * HD)
                mm = pe.matmul(ps[0:HD, 3, hs], stok[:, hs], w_small[0:HD, 3, :], start=True, stop=True)
            mm.then_inc(s("qkv_slices_made"), 1)
            pe.wait_ge(s("qkv_slices_ready"), 3)
            for h in range(H):
                hs = slice(h * HD, (h + 1) * HD)
                mm = pe.matmul(ps[0:HD, 4, hs], qT[:, hs], kT[:, hs], start=True, stop=True)
            mm.then_inc(s("scores_made"), 1)
            pe.wait_ge(s("attn_ready"), 1)
            for h in range(H):
                hs = slice(h * HD, (h + 1) * HD)
                mm = pe.transpose(ps[0:HD, 5, hs], attn[:, hs], ident[0:HD, 0:HD])
            mm.then_inc(s("attn_turned"), 1)
            pe.wait_ge(s("attnT_ready"), 1)
            for h in range(H):
                hs = slice(h * HD, (h + 1) * HD)
                mm = pe.matmul(ps[0:HD, 6, hs], vv[:, hs], attnT[:, hs], start=True, stop=True)
            mm.then_inc(s("os_made"), 1)
            pe.wait_ge(s("osT_ready"), 2)
            for h in range(H):
                mm = pe.matmul(ps[:, h // 2, 0:D], osT[:, h, :], w_out[:, h, :], start=(h % 2 == 0), stop=(h % 2 == 1))
            mm.then_inc(s("m_made"), 1)

            pe.wait_ge(s("m_ready"), 1)

            def out_step(i, par):
                t = live(i, 0)
                if t is not None:
                    pe.wait_ge(s("w_copied_back"), t + 1)
                    if not isinstance(t, int) or t >= 2:
                        pe.wait_ge(s("wT_ready"), t - 1)
                    for j in range(4):
                        mm = pe.transpose(ps[:, par, j * PT:(j + 1) * PT], wcopy_ring[:, par, j * P:(j + 1) * P], ident[0:PT, 0:PT])
                    mm.then_inc(s("w_turned"), 1)
                t = live(i, 1)
                if t is not None:
                    q = 1 - par
                    pe.wait_ge(s("wT_ready"), t + 1)
                    if not isinstance(t, int) or t >= 2:
                        pe.wait_ge(s("out_ready"), t - 1)
                    pe.matmul(ps[0:PT, 4 + q, 0:D], ones3[:, 0:PT], gbias3[0][:, :], start=True, stop=False)
                    for j in range(4):
                        mm = pe.matmul(ps[0:PT, 4 + q, 0:D], wT_ring[:, 4 * q + j, :], m_out[:, j, :], start=False, stop=(j == 3))
                    mm.then_inc(s("y_made"), 1)
            run_tiles(pe, None, out_step, NT, 1)

        @block.vector
        def _(dve):
            do = Order(dve, s("dve_order"))
            link = do.link

            dve.wait_ge(s("edges_loaded"), 64)
            dve.wait_ge(s("bin_id_set"), 1)
            link(dve.tensor_scalar(quot, e_src, 1.0 / NT, -0.49, ALU.mult, ALU.add))
            link(dve.scalar_tensor_tensor(out=bin16, in0=quot, scalar=-float(NT), in1=e_src, op0=ALU.mult, op1=ALU.add))
            link(dve.scalar_tensor_tensor(out=code, in0=quot, scalar=8192.0, in1=code, op0=ALU.mult, op1=ALU.add))
            with dve.Fori(0, NT) as b:
                do.enter(b, 1)
                link(dve.tensor_scalar(mask16, bin16, bin_id[:, bass.ds(b, 1)], None, ALU.is_equal, ALU.add,
                                       accum_out=counts[:, bass.ds(b, 1)]))
                do.leave(NT)
            dve.engine_nop().then_inc(s("counts_ready"), 1)
            dve.wait_ge(s("totals_made"), 1)
            link(dve.tensor_scalar(bins_i[:, :], ps[:, 7, 64:64 + NT], float(P - 1), None, ALU.add))
            link(dve.tensor_scalar(bins_i[:, :], bins_i[:, :], 7, None, ALU.arith_shift_right))
            link(dve.tensor_scalar(bins[:, 0, :], bins_i[:, :], float(P), None, ALU.mult))
            link(dve.tensor_tensor_scan(bins[:, 1, :], bins[:, 0, :], ones[:, 0:NT], 0.0, ALU.add, ALU.mult))
            dve.engine_nop().then_inc(s("ends_ready"), 1)
            link(dve.tensor_tensor(bins[:, 2, :], bins[:, 1, :], bins[:, 0, :], ALU.subtract))
            link(dve.scalar_tensor_tensor(out=carry[:, :], in0=ps[:, 7, 0:NT], scalar=-1.0, in1=bins[:, 2, :], op0=ALU.add, op1=ALU.add))
            for c0, c1 in ((0, PIECE1 * STG), (PIECE1 * STG, EC)):
                n = c1 - c0
                with dve.Fori(0, NT) as b:
                    do.enter(b, 4)
                    link(dve.tensor_scalar(mask16[:, c0:c1], bin16[:, c0:c1], bin_id[:, bass.ds(b, 1)], None, ALU.is_equal))
                    link(dve.tensor_tensor_scan(count_run[:, c0:c1], mask16[:, c0:c1], ones[:, 0:1].to_broadcast([P, n]),
                                                carry[:, bass.ds(b, 1)], ALU.add, ALU.mult))
                    dve.nop(nofuse=True)
                    link(dve.copy_predicated(pos_f[:, c0:c1], mask16[:, c0:c1], count_run[:, c0:c1]))
                    link(dve.tensor_scalar(carry[:, bass.ds(b, 1)], count_run[:, c1 - 1:c1], 1.0, None, ALU.mult))
                    do.leave(NT)
                link(dve.tensor_copy(pos_i[:, c0:c1], pos_f[:, c0:c1]))
                link(dve.tensor_scalar(quot[:, c0:c1], pos_i[:, c0:c1], 7, None, ALU.arith_shift_right))
                link(dve.tensor_scalar(pos_i[:, c0:c1], pos_i[:, c0:c1], P - 1, None, ALU.bitwise_and))
                dve.scalar_tensor_tensor(out=pos_i[:, c0:c1], in0=pos_i[:, c0:c1], scalar=float(NCH), in1=quot[:, c0:c1],
                                         op0=ALU.mult, op1=ALU.add).then_inc(s("positions"), 1)
                dve.wait_ge(s("positions"), 1 if c0 == 0 else 2)

            dve.wait_ge(s("ends_turned"), 1)
            link(dve.tensor_scalar(chunk_end[:, :], ps[0:NT, 6, 0:1], 1.0 / P, None, ALU.mult))
            dve.tensor_scalar(tcmp, tcmp, chunk_end[:, 0:1], None, ALU.is_ge).then_inc(s("tcmp_ready"), 1)
            dve.wait_ge(s("tiles_made"), 1)
            link(dve.tensor_scalar(tile_row.rearrange("p (k c) -> p k c", k=2), ps[0:1, 6:8, 0:NCH // 2], float(NT - 1), None, ALU.min))
            dve.sem_inc(s("tiles_kept"), 1)

            def split3(dst, src, n):
                part = [split_bf[:, k, 0:n] for k in range(3)]
                link(dve.tensor_copy(part[0], src))
                link(dve.tensor_tensor(split[:, 0, 0:n], src, part[0], ALU.subtract))
                link(dve.tensor_copy(part[1], split[:, 0, 0:n]))
                link(dve.tensor_tensor(split[:, 1, 0:n], split[:, 0, 0:n], part[1], ALU.subtract))
                link(dve.tensor_copy(part[2], split[:, 1, 0:n]))
                link(dve.tensor_scalar(split[:, 2, 0:n], part[0], ident[0:3, 0:1], None, ALU.mult))
                link(dve.scalar_tensor_tensor(out=split[:, 3, 0:n], in0=part[1], scalar=ident[0:3, 1:2], in1=split[:, 2, 0:n], op0=ALU.mult, op1=ALU.add))
                link(dve.scalar_tensor_tensor(out=dst, in0=part[2], scalar=ident[0:3, 2:3], in1=split[:, 3, 0:n], op0=ALU.mult, op1=ALU.add))
            dve.wait_ge(s("consts_set"), 1)
            dve.wait_ge(s("gw_loaded"), 64)
            for l in range(2):
                split3(gbias3[l][:, :], brow[:, l, :], D)
                dve.engine_nop().then_inc(s("gbias_ready"), 1)

            dve.wait_ge(s("small_loaded"), 14 * 16)
            link(dve.memset(wblock, 0.0))
            for j in range(6):
                link(dve.transpose(pw_turned[:, j, :], pw_stage[:, j, :]))
            for g in range(4):
                r = slice(32 * g, 32 * g + 32)
                link(dve.tensor_tensor(wblock[r, :, r], pw_turned[r, :, :], dw_stage[r, :, 2:3].to_broadcast([32, 6, 32]), ALU.mult))

            def mean_var(ready):
                mean_e, m2_e, mean_o, m2_o = (lnst[:, :, k] for k in (1, 2, 4, 5))
                link(dve.tensor_tensor(cols[:, 0, :], mean_e, mean_o, ALU.add))
                link(dve.tensor_scalar(mean[:, :], cols[:, 0, :], 0.5, None, ALU.mult))
                link(dve.tensor_tensor(cols[:, 1, :], mean_e, mean_o, ALU.subtract))
                link(dve.scalar_tensor_tensor(out=cols[:, 2, :], in0=cols[:, 1, :], scalar=0.25, in1=cols[:, 1, :], op0=ALU.mult, op1=ALU.mult))
                link(dve.tensor_tensor(cols[:, 3, :], m2_e, m2_o, ALU.add))
                link(dve.scalar_tensor_tensor(out=cols[:, 1, :], in0=cols[:, 3, :], scalar=1.0 / D, in1=cols[:, 2, :], op0=ALU.mult, op1=ALU.add))
                dve.tensor_scalar(cols[:, 0, :], cols[:, 1, :], LN_EPS, None, ALU.add).then_inc(s(ready), 1)
            dve.wait_ge(s("x_loaded"), 80)
            with dve.Fori(0, NT) as t:
                do.enter(t, 1)
                link(dve.bn_stats(lnst[:, bass.ds(t, 1), :], nodes[:, bass.ds(t, 1), :]))
                do.leave(NT)
            mean_var("xvar_ready")
            dve.wait_ge(s("xstd_ready"), 1)
            link(dve.reciprocal(cols[:, 2, :], cols[:, 1, :]))
            with dve.Fori(0, NT) as t:
                do.enter(t, 1)
                link(dve.tensor_scalar(nodes[:, bass.ds(t, 1), :], nodes[:, bass.ds(t, 1), :], mean[:, bass.ds(t, 1)],
                                       cols[:, 2, bass.ds(t, 1)], ALU.subtract, ALU.mult))
                do.leave(NT)
            dve.engine_nop().then_inc(s("xn_ready"), 1)

            c0, c1, c2, c3 = (cols[:, k, :] for k in range(4))
            link(dve.tensor_tensor(c3, c2, c2, ALU.mult))
            link(dve.scalar_tensor_tensor(out=c2, in0=c0, scalar=-LN_EPS, in1=c3, op0=ALU.add, op1=ALU.mult))
            dve.tensor_scalar(c0, c2, float(D), 1e-30, ALU.mult, ALU.max).then_inc(s("xnorm2_ready"), 1)
            dve.wait_ge(s("xnorm_ready"), 1)
            link(dve.tensor_scalar(c2, c1, MAXN, None, ALU.min))
            link(dve.tensor_scalar(c0, c2, 1.0, None, ALU.add))
            dve.tensor_scalar(c3, c2, -1.0, 1.0, ALU.mult, ALU.add).then_inc(s("log_args"), 1)
            dve.wait_ge(s("logs_ready"), 2)
            link(dve.tensor_tensor(c0, c0, c3, ALU.subtract))
            link(dve.tensor_scalar(fac[:, :], c0, 0.5, None, ALU.mult))
            link(dve.tensor_tensor(c3, c2, c2, ALU.mult))
            link(dve.tensor_scalar(c0, c3, 1.0 / 13, 1.0 / 11, ALU.mult, ALU.add))
            for k in (9, 7, 5, 3, 1):
                link(dve.tensor_tensor(c0, c0, c3, ALU.mult))
                link(dve.tensor_scalar(c0, c0, 1.0 / k, None, ALU.add))
            link(dve.tensor_tensor(c0, c0, c2, ALU.mult))
            link(dve.tensor_scalar(few[:, :], c2, 0.2, None, ALU.is_lt))
            link(dve.copy_predicated(fac[:, :], few[:, :], c0))
            link(dve.reciprocal(c3, c1))
            link(dve.tensor_tensor(fac[:, :], fac[:, :], c3, ALU.mult))
            def scale_step(i, par):
                t = live(i, 0)
                if t is not None:
                    if not isinstance(t, int) or t >= 2:
                        dve.wait_ge(s("scaled_used"), t - 1)
                    dve.tensor_scalar(hin[:, par:par + 1, :], nodes[:, bass.ds(t, 1), :], fac[:, bass.ds(t, 1)], None, ALU.mult).then_inc(s("scaled"), 1)
            run_tiles(dve, None, scale_step, NT, 0)
            dve.wait_ge(s("mu_ready"), 1)

            def centre_step(i, par):
                t = live(i, 0)
                if t is not None:
                    if not isinstance(t, int) or t >= 2:
                        dve.wait_ge(s("centred_used"), t - 1)
                    dve.scalar_tensor_tensor(out=hin[:, par:par + 1, :], in0=nodes[:, bass.ds(t, 1), :], scalar=fac[:, bass.ds(t, 1)],
                                             in1=mu[0:PT, :].unsqueeze(1), op0=ALU.mult, op1=ALU.subtract).then_inc(s("centred"), 1)
            run_tiles(dve, None, centre_step, NT, 0)
            dve.wait_ge(s("muT_ready"), 1)
            for k in range(2):
                link(dve.tensor_scalar(prod[:, 2 + k, :], wqkv[:, k, :], muT[:, k:k + 1], None, ALU.mult))
            dve.wait_ge(s("cw_made"), 1)
            for k in range(2):
                link(dve.tensor_tensor(prod[:, k, :].rearrange("p (a b) -> p a b", a=2), ps[:, 4 + 2 * k:6 + 2 * k, 0:CH3 // 2],
                                       wqkv[:, k, :].rearrange("p (a b) -> p a b", a=2), ALU.mult))
            dve.sem_inc(s("prods_ready"), 1)
            dve.wait_ge(s("bnsums_made"), 1)
            halves = lambda ap: ap.rearrange("p (a b) -> p a b", a=2)
            link(dve.tensor_scalar(halves(prod[:, 2, :]), ps[:, 2:4, 0:CH3 // 2], 1.0, None, ALU.mult))
            dve.tensor_scalar(halves(prod[:, 0, :]), ps[:, 0:2, 0:CH3 // 2], LN_EPS, None, ALU.add).then_inc(s("bnvar_ready"), 1)
            dve.wait_ge(s("bnstd_ready"), 1)
            link(dve.reciprocal(prod[:, 3, :], prod[:, 1, :]))
            link(dve.tensor_tensor(prod[:, 3, :], prod[:, 3, :], bn_gam, ALU.mult))
            link(dve.tensor_tensor(prod[:, 2, :], prod[:, 2, :], prod[:, 3, :], ALU.mult))
            link(dve.tensor_tensor(prod[:, 2, :], bn_bet, prod[:, 2, :], ALU.subtract))
            for k in range(2):
                link(dve.tensor_tensor(wqkv[:, k, :], wqkv[:, k, :], prod[:, 3, :], ALU.mult))
            split3(qbias3, prod[0:3, 2, :], CH3)
            dve.sem_inc(s("mixw_ready"), 1)

            def mix_step(i, par):
                q = 1 - par
                t = live(i, 0)
                if t is not None:
                    if not isinstance(t, int) or t >= 2:
                        dve.wait_ge(s("hin_turned"), t - 1)
                    dve.tensor_scalar(hin[:, par:par + 1, :], nodes[:, bass.ds(t, 1), :], fac[:, bass.ds(t, 1)], None, ALU.mult).then_inc(s("hin_ready"), 1)
                t = live(i, 2)
                if t is not None:
                    c = lambda k: sm[:, par, k:k + 1]
                    dve.wait_ge(s("on2_ready"), t + 1)
                    dve.tensor_scalar(c(15), c(3), 1e-30, None, ALU.max).then_inc(s("on2_clipped"), 1)
                    dve.wait_ge(s("on_ready"), t + 1)
                    link(dve.tensor_scalar(c(16), c(15), c(14), 1e-15, ALU.mult, ALU.max))
                    link(dve.reciprocal(c(17), c(16)))
                    link(dve.tensor_scalar(c(18), c(16), ATANH_MAXN, c(17), ALU.min, ALU.mult))
                    link(dve.tensor_tensor(c(19), c(18), c(14), ALU.mult))
                    dve.wait_ge(s("ft_made"), t + 1)
                    dve.scalar_tensor_tensor(out=mixo[:, bass.ds(t, 1), :], in0=ps[0:PT, 6, D:2 * D].unsqueeze(1), scalar=c(19),
                                             in1=bres.unsqueeze(1), op0=ALU.mult, op1=ALU.add).then_inc(s("ft_kept"), 1)
                t = live(i, 1)
                if t is not None:
                    c = lambda k: sm[:, q, k:k + 1]
                    dve.wait_ge(s("norms2_ready"), t + 1)
                    link(dve.tensor_scalar(c(5), c(0), 1e-30, None, ALU.max))
                    dve.tensor_tensor(c(6), c(5), c(1), ALU.add).then_inc(s("norms2_clipped"), 1)
                    part = cat[:, q, :].rearrange("p (g c) -> p g c", c=96)
                    e = [ev[:, k, :].rearrange("p (g c) -> p g c", c=32) for k in range(4)]
                    link(dve.tensor_scalar(e[0], part[:, :, 32:64], 0.0, None, ALU.max))
                    link(dve.tensor_reduce(ev[:, 1, 0:NG], e[0], AX.X, ALU.add))
                    link(dve.scalar_tensor_tensor(out=e[2], in0=part[:, :, 0:32], scalar=0.0,
                                                  in1=ev[:, 1, 0:NG].unsqueeze(2).to_broadcast([PT, NG, 32]), op0=ALU.max, op1=ALU.mult))
                    dve.wait_ge(s("norms_ready"), t + 1)
                    link(dve.reciprocal(c(7), c(5)))
                    link(dve.tensor_scalar(c(8), c(5), ATANH_MAXN, c(7), ALU.min, ALU.mult))
                    link(dve.tensor_scalar(c(9), c(6), c(8), 1e-15, ALU.mult, ALU.max))
                    link(dve.reciprocal(c(10), c(9)))
                    link(dve.tensor_scalar(c(11), c(9), ATANH_MAXN, c(10), ALU.min, ALU.mult))
                    link(dve.tensor_tensor(c(12), c(11), c(8), ALU.mult))
                    link(dve.reciprocal(c(13), c(12)))
                    link(dve.tensor_tensor(c(14), c(12), c(12), ALU.mult))
                    link(dve.tensor_scalar(c(13), c(13), 1e-15, None, ALU.mult))
                    link(dve.tensor_scalar(e[0], part[:, :, 64:96], c(13), None, ALU.add))
                    link(dve.reciprocal(ev[:, 1, :], ev[:, 0, :]))
                    link(dve.tensor_tensor(e[3], part[:, :, 64:96], e[1], ALU.mult))
                    if not isinstance(t, int) or t >= 2:
                        dve.wait_ge(s("o_turned"), t - 1)
                    dve.tensor_tensor(o_ring[:, q, :], ev[:, 2, :], ev[:, 3, :], ALU.mult).then_inc(s("o_ready"), 1)
            run_tiles(dve, do, mix_step, NT, 2)
            dve.wait_ge(s("mix_tiles_done"), 1)
            dve.tensor_scalar(c0, nf2[:, :], 1e-30, None, ALU.max).then_inc(s("fnorm2_ready"), 1)
            dve.wait_ge(s("ftanh_ready"), 1)
            link(dve.tensor_scalar(c2, c2, MAXN, None, ALU.min))
            link(dve.reciprocal(c3, c1))
            link(dve.tensor_tensor(nf2[:, :], c2, c3, ALU.mult))
            dve.wait_ge(s("x_back"), 80)
            with dve.Fori(0, NT) as t:
                do.enter(t, 1)
                mt = mixo[:, bass.ds(t, 1), :]
                link(dve.scalar_tensor_tensor(out=mt, in0=mt, scalar=nf2[:, bass.ds(t, 1)], in1=xback[:, bass.ds(t, 1), :], op0=ALU.mult, op1=ALU.add))
                do.leave(NT)

            dve.wait_ge(s("sorted_loaded"), 16)
            dve.tensor_scalar(s_dst, s_code, 8191, None, ALU.bitwise_and).then_inc(s("sorted_split"), 1)
            link(dve.tensor_scalar(s_code, s_code, 13, None, ALU.arith_shift_right))
            link(dve.memset(s_row[:, NCH:], float(P)))
            link(dve.tensor_copy(s_row[:, 0:NCH], s_code))

            for l in range(2):
                link(dve.memset(acc[:, :, :], 0.0))
                link(dve.memset(gat[:, :, D:257], 1.0))
                dve.engine_nop().then_inc(s("ring_free"), 1)
                dve.engine_nop().then_inc(s("agg_added_credit"), 1)

                def make_onehot(g, half):
                    for k in range(GRP):
                        ins = dve.tensor_scalar(onehot[:, GRP * half + k, :], iota_row[:, :],
                                                s_row[:, bass.ds(g * GRP + k, 1)], None, ALU.is_equal)
                    ins.then_inc(s("onehot_ready"), 1)

                def add_group(g, half, l=l):
                    _, tiles = nc.values_load_multi_w_load_instructions(
                        tile_row[0:1, bass.ds(g * GRP, GRP)], [mybir.EngineType.DVE], min_val=0, max_val=NT - 1)
                    for k in range(GRP):
                        n = g * GRP + (k + NCH * l)
                        dve.wait_ge(s("agg_made"), n + 1)
                        if not (isinstance(n, int) and n == 0):
                            dve.wait_ge(s("agg_added"), n)
                        at = acc[:, bass.ds(tiles[k], 1), :]
                        dve.tensor_tensor(at, ps[0:PT, k % 4, 0:257].unsqueeze(1), at, ALU.add).then_inc(s("agg_added"), 1)

                make_onehot(0, 0)
                make_onehot(1, 1)
                add_group(0, 0)
                with dve.Fori(0, NGRP // 2 - 1) as j:
                    make_onehot(j * 2 + 2, 0)
                    add_group(j * 2 + 1, 1)
                    make_onehot(j * 2 + 3, 1)
                    add_group(j * 2 + 2, 0)
                add_group(NGRP - 1, 1)
                dve.wait_ge(s("agg_added"), NCH * (l + 1))

                link(dve.tensor_scalar(cols[:, 3, :], acc[:, :, D], 1.0, None, ALU.max))
                link(dve.reciprocal(cols[:, 2, :], cols[:, 3, :]))

                def post_step(i, par, l=l):
                    t = live(i, 0)
                    if t is not None:
                        if not isinstance(t, int) or t >= 2:
                            dve.wait_ge(s("u_turned"), t + (NT * l - 1))
                        dve.scalar_tensor_tensor(out=u_ring[:, par:par + 1, :], in0=acc[:, bass.ds(t, 1), 0:D],
                                                 scalar=cols[:, 2, bass.ds(t, 1)], in1=nodes[:, bass.ds(t, 1), :],
                                                 op0=ALU.mult, op1=ALU.add).then_inc(s("u_ready"), 1)
                    t = live(i, 2)
                    if t is not None:
                        dve.wait_ge(s("h_kept"), t + (NT * l + 1))
                        dve.bn_stats(lnst[:, bass.ds(t, 1), :], acc[:, bass.ds(t, 1), 0:D]).then_inc(s("h_stats"), 1)
                run_tiles(dve, None, post_step, NT, 2)
                dve.wait_ge(s("h_stats"), NT * (l + 1))
                mean_var("hvar_ready")
                dve.wait_ge(s("hstd_ready"), l + 1)
                link(dve.reciprocal(cols[:, 2, :], cols[:, 1, :]))
                dve.wait_ge(s("h_kept"), NT * (l + 1))
                dve.wait_ge(s("gamma_loaded"), 32 * (l + 1))
                with dve.Fori(0, NT) as t:
                    do.enter(t, 1)
                    ht = acc[:, bass.ds(t, 1), 0:D]
                    link(dve.scalar_tensor_tensor(out=ht, in0=ht, scalar=mean[:, bass.ds(t, 1)], in1=gam.unsqueeze(1),
                                                  op0=ALU.subtract, op1=ALU.mult))
                    dve.scalar_tensor_tensor(out=ht, in0=ht, scalar=cols[:, 2, bass.ds(t, 1)], in1=bet.unsqueeze(1),
                                             op0=ALU.mult, op1=ALU.add).then_inc(s("z_ready"), 1)
                    do.leave(NT)
                dve.wait_ge(s("silu_done"), NT * (l + 1))
            with dve.Fori(0, NT) as t:
                do.enter(t, 1)
                nt = nodes[:, bass.ds(t, 1), :]
                link(dve.tensor_tensor(nt, acc[:, bass.ds(t, 1), 0:D], mixo[:, bass.ds(t, 1), :], ALU.add))
                do.leave(NT)
            dve.sem_inc(s("x2_ready"), 1)

            dve.wait_ge(s("ffn_loaded"), 80)
            link(dve.tensor_scalar(inv_temp[:, :], inv_temp[:, :], 0.1, 5.0, ALU.max, ALU.min))
            link(dve.reciprocal(inv_temp[:, :], inv_temp[:, :]))
            split3(gbias3[0][:, :], brow[:, 0, :], D)
            with dve.Fori(0, NT) as t:
                do.enter(t, 1)
                link(dve.bn_stats(lnst[:, bass.ds(t, 1), :], nodes[:, bass.ds(t, 1), :]))
                do.leave(NT)
            mean_var("yvar_ready")
            heads = lambda ap: ap.rearrange("p (h g) -> p h g", g=G)
            dve.wait_ge(s("wc_made"), 1)
            for k in range(2):
                for r in range(2):
                    link(dve.tensor_tensor(heads(wc[:, k, :])[:, r:H:2, :], heads(ps[:, 4 + 2 * r + k, :])[:, r:H:2, :],
                                           inv_temp[:, r:H:2].unsqueeze(2).to_broadcast([P, H // 2, G]), ALU.mult))
            dve.wait_ge(s("lb_made"), 1)
            lb = split[:, 0, 0:HG]
            link(dve.tensor_tensor(heads(lb), heads(ps[0:3, 3, :]), b_sl[:, :].unsqueeze(1).to_broadcast([3, H, G]), ALU.add))
            link(dve.tensor_tensor(heads(split[:, 1, 0:HG]), heads(lb), inv_temp[0:3, :].unsqueeze(2).to_broadcast([3, H, G]), ALU.mult))
            link(dve.tensor_copy(lbrow, split[:, 1, 0:HG]))
            split3(lbias3[:, :], lbrow, HG)
            dve.sem_inc(s("wc_ready"), 1)
            dve.wait_ge(s("ystd_ready"), 1)
            link(dve.reciprocal(c2, c1))
            dve.wait_ge(s("x2_stored"), 16)

            def slice_step(i, par):
                t = live(i, 0)
                if t is not None:
                    if not isinstance(t, int) or t >= 2:
                        dve.wait_ge(s("xl_turned"), t - 1)
                        dve.wait_ge(s("xl_copied"), t - 1)
                    dve.tensor_scalar(xl_ring[:, par:par + 1, :], nodes[:, bass.ds(t, 1), :], mean[:, bass.ds(t, 1)], cols[:, 2, bass.ds(t, 1)],
                                      ALU.subtract, ALU.mult).then_inc(s("xl_ready"), 1)
                t = live(i, 1)
                if t is not None:
                    q = 1 - par
                    dve.wait_ge(s("logits_made"), t + 1)
                    link(dve.tensor_reduce(head8[:, q, 0, :], heads(ps[0:PT, 4 + q, :]), AX.X, ALU.max))
                    dve.tensor_tensor(heads(ex_ring[:, q, :]), heads(ps[0:PT, 4 + q, :]), head8[:, q, 0, :].unsqueeze(2).to_broadcast([PT, H, G]),
                                      ALU.subtract).then_inc(s("shifted"), 1)
                t = live(i, 2)
                if t is not None:
                    dve.wait_ge(s("exp_done"), t + 1)
                    w = heads(ex_ring[:, par, :])
                    link(dve.tensor_reduce(head8[:, par, 1, :], w, AX.X, ALU.add))
                    link(dve.reciprocal(head8[:, par, 2, :], head8[:, par, 1, :]))
                    if not isinstance(t, int) or t >= 2:
                        dve.wait_ge(s("w_used"), t - 1)
                        dve.wait_ge(s("w_kept"), t - 1)
                    dve.tensor_tensor(heads(w_ring[:, par, :]), w, head8[:, par, 2, :].unsqueeze(2).to_broadcast([PT, H, G]), ALU.mult).then_inc(s("w_ready"), 1)
            run_tiles(dve, do, slice_step, NT, 2)

            dve.wait_ge(s("slices_summed"), 1)
            dve.wait_ge(s("w_kept"), NT)
            link(dve.tensor_scalar(rb[:, 0, :], ps[:, 0:4, D:D + 1].rearrange("p a b -> p (a b)"), 1e-5, None, ALU.add))
            link(dve.reciprocal(rb[:, 1, :], rb[:, 0, :]))
            for j in range(4):
                link(dve.tensor_scalar(tok[:, j, :], ps[:, j, 0:257], rb[:, 1, j:j + 1], None, ALU.mult))
            dve.sem_inc(s("tok_ready"), 1)
            dve.wait_ge(s("stok_made"), 1)
            dve.memset(osT, 0.0).then_inc(s("osT_zeroed"), 1)
            dve.wait_ge(s("scores_made"), 1)
            mx = head8[0:HD, 0, 0, :]
            link(dve.tensor_reduce(mx, heads(ps[0:HD, 4, :]), AX.X, ALU.max))
            dve.tensor_tensor(heads(attn), heads(ps[0:HD, 4, :]), mx.unsqueeze(2).to_broadcast([HD, H, G]), ALU.subtract).then_inc(s("scores_shifted"), 1)
            dve.wait_ge(s("scores_exp"), 1)
            link(dve.tensor_reduce(head8[0:HD, 0, 1, :], heads(attn), AX.X, ALU.add))
            link(dve.reciprocal(head8[0:HD, 0, 2, :], head8[0:HD, 0, 1, :]))
            dve.tensor_tensor(heads(attn), heads(attn), head8[0:HD, 0, 2, :].unsqueeze(2).to_broadcast([HD, H, G]), ALU.mult).then_inc(s("attn_ready"), 1)

            dve.wait_ge(s("x2_back"), 80)
            def out_step(i, par):
                t = live(i, 1)
                if t is not None:
                    q = 1 - par
                    dve.wait_ge(s("y_made"), t + 1)
                    xt = nodes[:, bass.ds(t, 1), :]
                    dve.tensor_tensor(xt, ps[0:PT, 4 + q, 0:D].unsqueeze(1), xt, ALU.add).then_inc(s("out_ready"), 1)
            run_tiles(dve, None, out_step, NT, 1)


def kernel(**inputs):
    import numpy as _np
    import concourse.bacc as _bacc
    from concourse import mybir as _mybir
    from concourse.bass_utils import run_bass_kernel_spmd as _run

    nc = _bacc.Bacc("TRN2", target_bir_lowering=False, num_devices=1)
    arrays, args = {}, {}
    for name, value in inputs.items():
        value = _np.ascontiguousarray(value)
        arrays[f"in_{name}_dram"] = value
        args[name] = nc.dram_tensor(f"in_{name}_dram", value.shape, _mybir.dt.from_np(value.dtype), kind="ExternalInput").ap()
    out = nc.dram_tensor("out_0_dram", (N, D), _mybir.dt.float32, kind="ExternalOutput").ap()
    gps_kernel(nc, args, out)
    r = _run(nc, [arrays], core_ids=[0])
    return r.results[0]["out_0_dram"]
```

```python
import concourse.bass as bass
from concourse import mybir
from contextlib import ExitStack

F32 = mybir.dt.float32
BF16 = mybir.dt.bfloat16
I32 = mybir.dt.int32
U16 = mybir.dt.uint16
ALU = mybir.AluOpType
ACT = mybir.ActivationFunctionType
AX = mybir.AxisListType

N, D = 6250, 256
P = 128
PT, NT = 125, 50
E = 100000
EC = 782
EPAD = P * EC - E
NCH = 832
GRP = 8
NGRP = NCH // GRP
STG = 17
UNR = 5
PIECE1 = 9
CH3 = 3 * D
NG = 16
H, HD, G = 8, 64, 64
HG = H * G
PADCODE = 1 << 20
LN_EPS = 1e-5
MAXN = 0.9999899864196777
ATANH_MAXN = 6.102372169494629


class Order:

    def __init__(self, eng, sem):
        self.eng, self.sem, self.count = eng, sem, 0

    def link(self, ins):
        ins.then_inc(self.sem, 1)
        self.count += 1
        self.eng.wait_ge(self.sem, self.count)

    def link_all(self, instructions):
        for ins in instructions:
            self.mark(ins)
        self.wait()

    def mark(self, ins):
        ins.then_inc(self.sem, 1)
        self.count += 1

    def wait(self):
        self.eng.wait_ge(self.sem, self.count)

    def turn(self):
        self.eng.sem_clear(self.sem)
        self.count = 0


def run_tiles(eng, order, step, n, lag):
    peel = lag + 2 + (lag % 2)
    for i in range(peel):
        step(i, i % 2)
    with eng.Fori(0, (n - peel) // 2) as j:
        if order:
            order.turn()
        step(j * 2 + peel, 0)
        step(j * 2 + (peel + 1), 1)
    for i in range(n, n + lag):
        step(i, i % 2)


def live(i, lag, n=NT):
    if isinstance(i, int):
        return i - lag if 0 <= i - lag < n else None
    return i - lag


def gps_kernel(nc, a, out):
    ctx = ExitStack()
    with ctx:
        def sb(name, shape, dt=F32):
            return ctx.enter_context(nc.sbuf_tensor(name, shape, dt))

        def sem(name):
            return ctx.enter_context(nc.semaphore(name))

        x_d = a["x"].rearrange("(p t) c -> p t c", t=NT)
        out_d = out.rearrange("(p t) c -> p t c", t=NT)
        table = [nc.dram_tensor(f"table{l}", (N, D), F32, kind="Internal").ap() for l in range(2)]
        table_d = [t.rearrange("(p t) c -> p t c", t=NT) for t in table]
        x2_dram = nc.dram_tensor("x2_rows", (N, D), F32, kind="Internal").ap()
        x2_d = x2_dram.rearrange("(p t) c -> p t c", t=NT)
        sorted_dram = nc.dram_tensor("sorted_edges", (P * NCH, 1), I32, kind="Internal").ap()
        sorted_rows = sorted_dram.rearrange("(p c) o -> p (c o)", p=P)

        nodes = sb("nodes", [PT, NT, D])
        big = sb("big", [P, NT * 257 + NT * D])
        acc = big[0:PT, 0:NT * 257].rearrange("p (t c) -> p t c", c=257)
        mixo = big[0:PT, NT * 257:].rearrange("p (t c) -> p t c", c=D)
        arena_a = sb("arena_a", [P, 4750])
        arena_b = sb("arena_b", [P, 16 * 257 + 2 * GRP * PT])

        def carve(arena, at, shape, dt=F32, parts=P):
            n = 1
            for s in shape:
                n *= s
            words = n if dt in (F32, I32) else (n + 1) // 2
            v = arena[0:parts, at:at + words]
            if dt != F32:
                v = v.bitcast(dt)
            if len(shape) == 2:
                v = v.rearrange("p (a b) -> p a b", b=shape[1])
            elif len(shape) == 3:
                v = v.rearrange("p (a b c) -> p a b c", b=shape[1], c=shape[2])
            return v, at + words

        e_src, o = carve(arena_a, 0, [EC], I32)
        code, o = carve(arena_a, o, [EC], I32)
        quot, o = carve(arena_a, o, [EC], I32)
        count_run = quot.bitcast(F32)
        pos_f, o = carve(arena_a, o, [EC])
        bin16, o = carve(arena_a, o, [EC], U16)
        mask16, o = carve(arena_a, o, [EC], U16)
        pos_i = e_src
        spare16 = [mask16] + [v.bitcast(U16)[:, k * EC:(k + 1) * EC] for v in (pos_f, quot) for k in range(2)]
        tile_row, o = carve(arena_a, o, [NCH], I32, 1)
        s_code, o = carve(arena_a, 0, [NCH], I32)
        s_dst, o = carve(arena_a, o, [NCH], I32)
        s_row, o = carve(arena_a, o, [NCH])
        away, o = carve(arena_a, o, [GRP, PT])
        x_tile, o = carve(arena_a, o, [D], F32, PT)
        assert o <= 4750 - NCH
        fill, _ = carve(arena_b, 0, [NCH], I32)
        tcmp, _ = carve(arena_b, NCH, [NCH], F32, NT)
        triu, _ = carve(arena_b, 2 * NCH, [P])
        wstage, _ = carve(arena_b, 2 * NCH + P, [2, 2, D])
        gat, o = carve(arena_b, 0, [16, 257])
        onehot, o = carve(arena_b, o, [2 * GRP, PT])
        u_ring, o = carve(arena_b, 0, [2, D], F32, PT)
        uT_ring, o = carve(arena_b, o, [4, PT])
        gam, o = carve(arena_b, 16 * 257 + 2 * GRP * PT - 2 * D, [D], F32, PT)
        bet, o = carve(arena_b, o, [D], F32, PT)
        pos_stage = sb("pos_stage", [P, 2, STG], I32)
        code_stage = sb("code_stage", [P, 2, STG], I32)
        dst_stage = sb("dst_stage", [P, 2, GRP], I32)

        ident = sb("ident", [P, P])
        ones = sb("ones", [P, P])
        iota_row = sb("iota_row", [P, PT])
        bin_id = sb("bin_id", [P, NT])
        counts = sb("counts", [P, NT])
        carry = sb("carry", [P, NT])
        bins = sb("bins", [P, 3, NT])
        bins_i = sb("bins_i", [P, NT], I32)
        chunk_end = sb("chunk_end", [NT, 1])
        ones3 = sb("ones3", [3, P], BF16)
        lnst = sb("lnst", [PT, NT, 6])
        mean = sb("mean", [PT, NT])
        cols = sb("cols", [PT, 4, NT])
        wT = [sb(f"w{l}T", [P, 2, D]) for l in range(2)]
        gbias3 = [sb(f"gbias3_{l}", [3, D], BF16) for l in range(2)]
        rT_ring, wa = carve(big, 0, [2, 6, PT])
        ev, wa = carve(big, wa, [4, NG * 32], F32, PT)
        junk, wa = carve(big, wa, [2, CH3], F32, PT)
        brow, wb = carve(big, 0, [2, D], F32, 3)
        split, wb = carve(big, wb, [4, CH3], F32, 3)
        split_bf, wb = carve(big, wb, [3, CH3], BF16, 3)
        assert wb <= wa
        wqkv, wa = carve(big, wa, [2, CH3])
        wqkv_flat = big[:, wa - 2 * CH3:wa]
        wblock, wa = carve(big, wa, [6, P])
        wres, wa = carve(big, wa, [4, D])
        wres_flat = big[:, wa - 4 * D:wa]
        bres, wa = carve(big, wa, [D], F32, PT)
        qbias3, wa = carve(big, wa, [CH3], BF16, 3)
        wres_stage, wa = carve(big, wa, [2, 2 * D])
        bn_gam, wa = carve(big, wa, [CH3])
        bn_bet, wa = carve(big, wa, [CH3])
        pw_stage, wa = carve(big, wa, [6, 32])
        pw_turned, wa = carve(big, wa, [6, 32])
        dw_stage, wa = carve(big, wa, [6, 5])
        hin, wa = carve(big, wa, [2, D], F32, PT)
        assert wa <= NT * 257
        wq_stage, wa = carve(big, NT * 257, [6, 5 * D])
        prod, wa = carve(big, wa, [4, CH3])
        cov, wa = carve(big, wa, [2, D])
        mu, wa = carve(big, wa, [D])
        muT, wa = carve(big, wa, [2])
        assert wa <= NT * 257 + NT * D
        cat, o = carve(arena_b, 0, [2, 2 * CH3], F32, PT)
        o_ring, o = carve(arena_b, o, [2, 2 * D], F32, PT)
        oT_ring, o = carve(arena_b, o, [8, PT])
        hT_ring, o = carve(arena_b, o, [4, PT])
        assert o <= 16 * 257 + 2 * GRP * PT
        ffw = big[0:PT, 0:NT * HG].rearrange("p (t c) -> p t c", c=HG)
        w_fx, o = carve(arena_a, 0, [2, HG])
        w_out, o = carve(arena_a, o, [H, D], F32, HD)
        wx_stage, o = carve(arena_a, o, [2, HG])
        beta_row = arena_a[0:1, o - 2 * HG:o - HG]
        b_fx, o = carve(arena_a, o, [HG], F32, 1)
        wc, o = carve(arena_b, 0, [2, HG])
        wxT_flat = arena_b[:, o:o + 4 * D]
        wxT, o = carve(arena_b, o, [4, D])
        xlT_ring, o = carve(arena_b, o, [4, PT])
        ex_ring, o = carve(arena_b, o, [2, HG], F32, PT)
        w_ring, o = carve(arena_b, o, [2, HG], F32, PT)
        xl_ring, o = carve(arena_b, o, [2, D], F32, PT)
        assert o <= 16 * 257 + 2 * GRP * PT - 2 * D
        wT_ring, o = carve(arena_b, 0, [8, PT])
        wcopy_ring, o = carve(arena_b, o, [2, HG], F32, PT)
        m_out, _ = carve(arena_b, 16 * 257 + 2 * GRP * PT - 4 * D, [4, D])
        tok, o = carve(arena_b, 0, [4, 257])
        tokT, o = carve(arena_b, o, [2, HG])
        osT = tokT.rearrange("p a b -> p (a b)")[0:HD, :].rearrange("p (h c) -> p h c", c=P)
        stok, o = carve(arena_b, o, [HG], F32, HD)
        attnT = stok
        qT, o = carve(arena_b, o, [HG], F32, HD)
        kT, o = carve(arena_b, o, [HG], F32, HD)
        vv, o = carve(arena_b, o, [HG], F32, HD)
        attn, o = carve(arena_b, o, [HG], F32, HD)
        assert o <= 16 * 257 + 2 * GRP * PT - 4 * D
        lbrow = brow.rearrange("p a b -> p (a b)")
        w_small = sb("w_small", [P, 4, HD])
        b_x8 = sb("b_x8", [H, HD])
        b_x8T = sb("b_x8T", [HD, H])
        b_sl = sb("b_sl", [3, G])
        inv_temp = sb("inv_temp", [P, H])
        lbias3 = sb("lbias3", [3, HG], BF16)
        head8 = sb("head8", [PT, 2, 3, H])
        fac = sb("fac", [PT, NT])
        nf2 = sb("nf2", [PT, NT])
        few = sb("few", [PT, NT], I32)
        sm = sb("sm", [PT, 2, 20])
        rb = sb("rb", [P, 2, 4])

        ps = ctx.enter_context(nc.psum_tensor("ps", [P, 8, 512], F32))

        sems = {}

        def s(name):
            if name not in sems:
                sems[name] = sem(name)
            return sems[name]

        block = ctx.enter_context(nc.Block())

        @block.sync
        def _(sp):
            sp.wait_ge(s("edges_padded"), 1)
            for src, dst in ((a["src"], e_src), (a["dst"], code)):
                full = (P - 1) * EC
                sp.dma_start(dst[0:P - 1, :], src[0:full].rearrange("(p c) -> p c", c=EC)).then_inc(s("edges_loaded"), 16)
                sp.dma_start(dst[P - 1:P, 0:EC - EPAD], src[full:E].rearrange("(p c) -> p c", p=1)).then_inc(s("edges_loaded"), 16)
            for k in range(5):
                sp.dma_start(nodes[:, 10 * k:10 * k + 10, :], x_d[:, 10 * k:10 * k + 10, :]).then_inc(s("x_loaded"), 16)
            sp.dma_start(wq_stage, a["L0_mix_w_qkv"].rearrange("(j p) c k -> p j (c k)", p=P)).then_inc(s("wq_loaded"), 16)
            sp.wait_ge(s("fill_set"), 1)
            sp.dma_start(sorted_rows, fill[:, :]).then_inc(s("sorted_cleared"), 16)
            sp.wait_ge(s("xn_ready"), 1)
            sp.dma_start(table_d[0], nodes[:, :, :]).then_inc(s("table0_stored"), 16)
            sp.wait_ge(s("scattered0"), 16 * STG * (EC // STG // 2))
            sp.wait_ge(s("scattered1"), 16 * STG * (EC // STG // 2))
            sp.dma_start(s_code, sorted_rows).then_inc(s("sorted_loaded"), 16)
            sp.dma_start(x_tile, x_d[:, 0, :]).then_inc(s("x_tile_loaded"), 16)
            with sp.Fori(1, NT) as t:
                sp.wait_ge(s("x_tile_used"), t)
                sp.dma_start(x_tile.unsqueeze(1), x_d[:, bass.ds(t, 1), :]).then_inc(s("x_tile_loaded"), 16)
            for l in range(2):
                sp.wait_ge(s("agg_added"), NCH * (l + 1))
                sp.dma_start(gam, a[f"L0_gnn_g{l}"].partition_broadcast(PT)).then_inc(s("gamma_loaded"), 16)
                sp.dma_start(bet, a[f"L0_gnn_beta{l}"].partition_broadcast(PT)).then_inc(s("gamma_loaded"), 16)
                if l == 1:
                    ffn = lambda name: a[f"L0_ffn_{name}"]
                    for dst, src in ((wx_stage, ffn("W_x").rearrange("(k p) n -> p k n", p=P)),
                                     (w_fx, ffn("W_fx").rearrange("(k p) n -> p k n", p=P)),
                                     (w_out, ffn("W_out").rearrange("(h c) n -> c h n", c=HD)),
                                     (b_fx, ffn("b_fx").rearrange("(o n) -> o n", o=1))):
                        sp.dma_start(dst, src).then_inc(s("ffn_loaded"), 16)
                if l == 0:
                    for k in range(5):
                        sp.wait_ge(s("silu_done"), 10 * (k + 1))
                        sp.dma_start(table_d[1][:, 10 * k:10 * k + 10, :], nodes[:, 10 * k:10 * k + 10, :]).then_inc(s("table1_stored"), 16)
            for k in range(5):
                sp.wait_ge(s("x2_summed"), 10 * (k + 1))
                sp.dma_start(x2_d[:, 10 * k:10 * k + 10, :], nodes[:, 10 * k:10 * k + 10, :]).then_inc(s("x2_stored"), 16)
                if k == 0:
                    sp.dma_start(brow[:, 0, :], a["L0_ffn_b_out"].partition_broadcast(3)).then_inc(s("b_out_loaded"), 16)
            sp.wait_ge(s("slices_summed"), 1)
            for k in range(5):
                sp.dma_start(nodes[:, 10 * k:10 * k + 10, :], x2_d[:, 10 * k:10 * k + 10, :]).then_inc(s("x2_back"), 16)
            for k in range(5):
                sp.wait_ge(s("out_ready"), 10 * (k + 1))
                sp.dma_start(out_d[:, 10 * k:10 * k + 10, :], nodes[:, 10 * k:10 * k + 10, :]).then_inc(s("out_stored"), 16)
            sp.wait_ge(s("out_stored"), 80)
            sp.wait_ge(s("table0_stored"), 16)
            sp.wait_ge(s("table1_stored"), 80)
            sp.wait_ge(s("x2_stored"), 80)

        @block.gpsimd
        def _(pool):
            po = Order(pool, s("pool_order"))
            iota = dict(base=0, channel_multiplier=0, allow_small_or_imprecise_dtypes=True)
            po.link(pool.memset(e_src[96:P, EC - EPAD:EC], 0))
            po.link(pool.memset(code[96:P, EC - EPAD:EC], PADCODE))
            pool.sem_inc(s("edges_padded"), 1)
            po.link(pool.iota(bin_id[:, :], [[1, NT]], **iota))
            pool.sem_inc(s("bin_id_set"), 1)
            po.link(pool.memset(fill[:, :], PADCODE))
            pool.sem_inc(s("fill_set"), 1)
            po.link(pool.memset(ones[:, :], 1.0))
            po.link(pool.memset(ones3[:, :], 1.0))
            po.link(pool.affine_select(out=triu[:, :], in_=ones[:, :], compare_op=ALU.is_gt, fill=0.0, base=0,
                                       pattern=[[1, P]], channel_multiplier=-1))
            po.link(pool.memset(ident[:, :], 0.0))
            po.link(pool.affine_select(out=ident[:, :], in_=ident[:, :], compare_op=ALU.not_equal, fill=1.0, base=0,
                                       pattern=[[-1, P]], channel_multiplier=1))
            po.link(pool.iota(iota_row[:, :], [[1, PT]], **iota))
            po.link(pool.iota(tcmp, [[1, NCH]], **iota))
            pool.sem_inc(s("consts_set"), 1)

            def scatter_batch(b, half, first):
                if not first:
                    pool.wait_ge(s(f"scattered{half}"), b[0] * (16 * STG))
                c0 = (b[0] * 2 + half) * STG
                pool.tensor_copy(pos_stage[:, half, :], pos_i[:, bass.ds(c0, STG)]).then_inc(s("staged"), 1)
                pool.wait_ge(s("staged"), (b[0] * 2 + half) * 2 + 1)
                pool.nop(nofuse=True)
                pool.tensor_copy(code_stage[:, half, :], code[:, bass.ds(c0, STG)]).then_inc(s("staged"), 1)
                pool.wait_ge(s("staged"), (b[0] * 2 + half) * 2 + 2)
                pool.nop(nofuse=True)
                for k in range(STG):
                    pool.indirect_dma_start(
                        sorted_dram, bass.IndirectOffsetOnAxis(ap=pos_stage[:, half, k:k + 1], axis=0),
                        code_stage[:, half, k:k + 1], None).then_inc(s(f"scattered{half}"), 16)

            pool.wait_ge(s("positions"), 1)
            pool.wait_ge(s("sorted_cleared"), 16)
            for half in range(2):
                scatter_batch([0], half, True)
            with pool.Fori(1, PIECE1 // 2) as j:
                for half in range(2):
                    scatter_batch([j], half, False)
            pool.wait_ge(s("positions"), 2)
            with pool.Fori(PIECE1 // 2, EC // STG // 2) as j:
                for half in range(2):
                    scatter_batch([j], half, False)

            def gather_group(l, j, half, first):
                if not first:
                    pool.wait_ge(s("agg_made"), (j * 2 + half) * GRP + (NCH * l - GRP))
                pool.wait_ge(s("dst_staged"), (j * 2 + half) + (NGRP * l + 1))
                pool.nop(nofuse=True)
                for k in range(GRP):
                    pool.indirect_dma_start(
                        gat[:, GRP * half + k, 0:D], None, table[l],
                        bass.IndirectOffsetOnAxis(ap=dst_stage[:, half, k:k + 1], axis=0)).then_inc(s(f"gathered{half}"), 16)

            for l in range(2):
                if l == 0:
                    pool.wait_ge(s("sorted_split"), 1)
                    pool.wait_ge(s("ring_free"), 1)
                    pool.wait_ge(s("table0_stored"), 16)
                else:
                    pool.wait_ge(s("ring_free"), 2)
                    pool.wait_ge(s("table1_stored"), 80)
                for half in range(2):
                    gather_group(l, 0, half, True)
                with pool.Fori(1, NGRP // 2) as j:
                    for half in range(2):
                        gather_group(l, j, half, False)

        @block.scalar
        def _(act):
            ao = Order(act, s("act_order"))
            for l in range(2):
                act.dma_start(wstage[:, l, :, :], a[f"L0_gnn_W{l}"].rearrange("(b p) d -> p b d", p=P)).then_inc(s("gw_loaded"), 16)
                act.dma_start(brow[:, l, :], a[f"L0_gnn_b{l}"].partition_broadcast(3)).then_inc(s("gw_loaded"), 16)
            mix = lambda name: a[f"L0_mix_{name}"]
            ffn = lambda name: a[f"L0_ffn_{name}"]
            for dst, src in ((wres_stage, mix("w_res").rearrange("(b p) c k -> p b (c k)", p=P)),
                             (pw_stage, mix("w_pw").rearrange("(j p) c k -> p j (c k)", p=P)),
                             (dw_stage, mix("w_dw").rearrange("(j p) c k -> p j (c k)", p=P)),
                             (bn_gam, mix("bn_gamma").partition_broadcast(P)),
                             (bn_bet, mix("bn_beta").partition_broadcast(P)),
                             (bres, mix("b_res").partition_broadcast(PT)),
                             (w_small[0:HD, 0, :], ffn("W_slice")),
                             (w_small[HD:P, 0, :], ffn("W_slice")),
                             (w_small[0:HD, 1, :], ffn("W_q")),
                             (w_small[0:HD, 2, :], ffn("W_k")),
                             (w_small[0:HD, 3, :], ffn("W_v")),
                             (b_x8[:, :], ffn("b_x").rearrange("(h c) -> h c", c=HD)),
                             (b_sl[:, :], ffn("b_slice").partition_broadcast(3)),
                             (inv_temp[:, :], ffn("temperature").rearrange("a h b c -> (a h b c)").partition_broadcast(P))):
                act.dma_start(dst, src).then_inc(s("small_loaded"), 16)
            for l in range(2):
                act.wait_ge(s("gw_turned"), l + 1)
                for k in range(2):
                    act.activation(wT[l][:, k, :], ps[:, 4 + l, k * D:(k + 1) * D], ACT.Copy).then_inc(s("gw_ready"), 1)
            for b in range(5):
                act.wait_ge(s("mw_turned"), b + 1)
                dst = wqkv_flat[:, b * 512:(b + 1) * 512] if b < 3 else wres_flat[:, (b - 3) * 512:(b - 2) * 512]
                act.activation(dst, ps[:, b, :], ACT.Copy).then_inc(s("mw_ready"), 1)
            act.wait_ge(s("xvar_ready"), 1)
            act.activation(cols[:, 1, :], cols[:, 0, :], ACT.Sqrt).then_inc(s("xstd_ready"), 1)

            act.wait_ge(s("xnorm2_ready"), 1)
            act.activation(cols[:, 1, :], cols[:, 0, :], ACT.Sqrt).then_inc(s("xnorm_ready"), 1)
            act.wait_ge(s("log_args"), 1)
            act.activation(cols[:, 0, :], cols[:, 0, :], ACT.Ln).then_inc(s("logs_ready"), 1)
            act.activation(cols[:, 3, :], cols[:, 3, :], ACT.Ln).then_inc(s("logs_ready"), 1)
            act.wait_ge(s("means_summed"), 1)
            act.activation(mu, ps[:, 0, 0:D], ACT.Copy, scale=1.0 / N).then_inc(s("mu_ready"), 1)
            act.wait_ge(s("mu_turned"), 1)
            act.activation(muT.unsqueeze(2), ps[:, 3, 0:2 * P].rearrange("p (k c) -> p k c", k=2)[:, :, 0:1], ACT.Copy).then_inc(s("muT_ready"), 1)
            act.wait_ge(s("gram_made"), 1)
            act.activation(cov, ps[:, 1:3, 0:D], ACT.Copy, scale=1.0 / N).then_inc(s("cov_ready"), 1)
            act.wait_ge(s("bnvar_ready"), 1)
            act.activation(prod[:, 1, :], prod[:, 0, :], ACT.Sqrt).then_inc(s("bnstd_ready"), 1)

            act.wait_ge(s("sorted_cleared"), 16)

            def mix_step(i, par):
                q = 1 - par
                t = live(i, 4)
                if t is not None:
                    act.wait_ge(s("ft_made"), t + 1)
                    act.activation(mixo[:, bass.ds(t, 1), :], ps[0:PT, 6, D:2 * D].unsqueeze(1), ACT.Copy).then_inc(s("ft_out"), 1)
                t = live(i, 0)
                if t is not None:
                    act.wait_ge(s("hin_turned"), t + 1)
                    if not isinstance(t, int) or t >= 2:
                        act.wait_ge(s("qkv_made"), t - 1)
                    act.activation(hT_ring[:, 2 * par:2 * par + 2, :], ps[:, 6, 0:2 * PT].rearrange("p (k c) -> p k c", k=2), ACT.Copy).then_inc(s("hT_ready"), 1)
                t = live(i, 1)
                if t is not None:
                    act.wait_ge(s("r_turned"), t + 1)
                    if not isinstance(t, int) or t >= 2:
                        act.wait_ge(s("s_made"), t - 1)
                    act.activation(rT_ring[:, q, :, :].rearrange("p (a b) c -> p a (b c)", a=2), ps[:, 4:6, 0:3 * PT], ACT.Copy).then_inc(s("rT_ready"), 1)
                t = live(i, 3)
                if t is not None:
                    act.wait_ge(s("o_turned"), t + 1)
                    if not isinstance(t, int) or t >= 2:
                        act.wait_ge(s("ft_made"), t - 1)
                    act.activation(oT_ring[:, 4 * q:4 * q + 4, :], ps[:, 7, 0:4 * PT].rearrange("p (k c) -> p k c", k=4), ACT.Copy).then_inc(s("oT_ready"), 1)
                    ao.link(act.activation(junk[:, 0, 0:2 * D], o_ring[:, q, :], ACT.Square, accum_out=sm[:, q, 3:4]))
                    act.sem_inc(s("on2_ready"), 1)
                t = live(i, 1)
                if t is not None:
                    act.wait_ge(s("s_made"), t + 1)
                    ao.link(act.activation(cat[:, q, CH3:].rearrange("p (a b) -> p a b", a=2), ps[0:PT, 2:4, 0:CH3 // 2], ACT.Copy))
                    act.sem_inc(s("s_kept"), 1)
                    ao.link(act.activation(junk[:, 1, :], cat[:, q, CH3:], ACT.Square, accum_out=sm[:, q, 1:2]))
                    act.sem_inc(s("norms2_ready"), 1)
                    act.wait_ge(s("norms2_clipped"), t + 1)
                    act.activation(sm[:, q, 5:7], sm[:, q, 5:7], ACT.Sqrt).then_inc(s("norms_ready"), 1)
                t = live(i, 3)
                if t is not None:
                    act.wait_ge(s("on2_clipped"), t + 1)
                    act.activation(sm[:, q, 15:16], sm[:, q, 15:16], ACT.Sqrt).then_inc(s("on_ready"), 1)
                t = live(i, 0)
                if t is not None:
                    act.wait_ge(s("qkv_made"), t + 1)
                    if not isinstance(t, int) or t >= 2:
                        act.wait_ge(s("o_ready"), t - 1)
                    ao.link(act.activation(cat[:, par, 0:CH3].rearrange("p (a b) -> p a b", a=2), ps[0:PT, 0:2, 0:CH3 // 2], ACT.Relu))
                    act.sem_inc(s("relu_done"), 1)
                    ao.link(act.activation(junk[:, 0, :], cat[:, par, 0:CH3], ACT.Square, accum_out=sm[:, par, 0:1]))
                t = live(i, 5)
                if t is not None:
                    act.wait_ge(s("ft_kept"), t + 1)
                    ao.link(act.activation(junk[:, 1, 0:D].unsqueeze(1), mixo[:, bass.ds(t, 1), :], ACT.Square, accum_out=nf2[:, bass.ds(t, 1)]))
            run_tiles(act, ao, mix_step, NT, 5)
            act.sem_inc(s("mix_tiles_done"), 1)
            act.wait_ge(s("fnorm2_ready"), 1)
            ao.link(act.activation(cols[:, 1, :], cols[:, 0, :], ACT.Sqrt))
            act.activation(cols[:, 2, :], cols[:, 1, :], ACT.Tanh).then_inc(s("ftanh_ready"), 1)

            for l in range(2):
                def stage_rows(j, half, first, l=l):
                    if not first:
                        act.wait_ge(s(f"gathered{half}"), (j + NGRP // 2 * l) * (16 * GRP))
                    act.activation(dst_stage[:, half, :], s_dst[:, bass.ds((j * 2 + half) * GRP, GRP)], ACT.Copy).then_inc(s("dst_staged"), 1)

                def make_onehot(j, half, first, l=l):
                    if not first:
                        act.wait_ge(s("agg_made"), (j * 2 + half) * GRP + (NCH * l - GRP))
                    for k in range(GRP):
                        ins = act.activation(away[:, k, :], iota_row[:, :], ACT.Abs, bias=s_row[:, bass.ds((j * 2 + half) * GRP + k, 1)])
                    ao.link(ins)
                    ao.link(act.activation(onehot[:, GRP * half:GRP * (half + 1), :], away, ACT.Relu, scale=-1.0, bias=ones[:, 0:1]))
                    act.sem_inc(s("onehot_ready"), 1)
                act.wait_ge(s("sorted_split"), 1)
                for half in range(2):
                    stage_rows(0, half, l == 0)
                act.wait_ge(s("ring_free"), l + 1)
                for half in range(2):
                    make_onehot(0, half, l == 0)
                with act.Fori(1, NGRP // 2) as j:
                    ao.turn()
                    for half in range(2):
                        stage_rows(j, half, False)
                        make_onehot(j, half, False)

                def post_step(i, par, l=l):
                    t = live(i, 0)
                    if t is not None:
                        act.wait_ge(s("u_turned"), t + (NT * l + 1))
                        if not isinstance(t, int) or t >= 2:
                            act.wait_ge(s("h_made"), t + (NT * l - 1))
                        act.activation(uT_ring[:, 2 * par:2 * par + 2, :],
                                       ps[:, 4 + par, 0:D].rearrange("p (k c) -> p k c", k=2)[:, :, 0:PT],
                                       ACT.Copy).then_inc(s("uT_ready"), 1)
                    t = live(i, 1)
                    if t is not None:
                        act.wait_ge(s("h_made"), t + (NT * l + 1))
                        act.activation(acc[:, bass.ds(t, 1), 0:D], ps[0:PT, 6 + 1 - par, 0:D].unsqueeze(1),
                                       ACT.Copy).then_inc(s("h_kept"), 1)
                run_tiles(act, None, post_step, NT, 1)
                if l == 1:
                    for b in range(2):
                        act.wait_ge(s("wx_turned"), b + 1)
                        act.activation(wxT_flat[:, b * 512:(b + 1) * 512], ps[:, b, :], ACT.Copy).then_inc(s("wxT_ready"), 1)
                    act.wait_ge(s("bx_turned"), 1)
                    act.activation(b_x8T[:, :], ps[0:HD, 2, 0:H], ACT.Copy).then_inc(s("bxT_ready"), 1)
                act.wait_ge(s("hvar_ready"), l + 1)
                act.activation(cols[:, 1, :], cols[:, 0, :], ACT.Sqrt).then_inc(s("hstd_ready"), 1)

                def silu_tile(t, l=l):
                    act.wait_ge(s("z_ready"), t + (NT * l + 1))
                    dst = nodes[:, bass.ds(t, 1), :] if l == 0 else acc[:, bass.ds(t, 1), 0:D]
                    act.activation(dst, acc[:, bass.ds(t, 1), 0:D], ACT.Silu).then_inc(s("silu_done"), 1)
                for k in range(UNR):
                    silu_tile(k)
                with act.Fori(1, NT // UNR) as g:
                    for k in range(UNR):
                        silu_tile(g * UNR + k)

            act.wait_ge(s("yvar_ready"), 1)
            act.activation(cols[:, 1, :], cols[:, 0, :], ACT.Sqrt).then_inc(s("ystd_ready"), 1)

            def slice_step(i, par):
                q = 1 - par
                t = live(i, 0)
                if t is not None:
                    act.wait_ge(s("xl_ready"), t + 1)
                    act.activation(nodes[:, bass.ds(t, 1), :], xl_ring[:, par:par + 1, :], ACT.Copy).then_inc(s("xl_copied"), 1)
                    act.wait_ge(s("xl_turned"), t + 1)
                    if not isinstance(t, int) or t >= 2:
                        act.wait_ge(s("logits_made"), t - 1)
                    act.activation(xlT_ring[:, 2 * par:2 * par + 2, :], ps[:, 6 + par, 0:2 * PT].rearrange("p (k c) -> p k c", k=2), ACT.Copy).then_inc(s("xlT_ready"), 1)
                t = live(i, 1)
                if t is not None:
                    act.wait_ge(s("shifted"), t + 1)
                    act.activation(ex_ring[:, q, :], ex_ring[:, q, :], ACT.Exp).then_inc(s("exp_done"), 1)
                t = live(i, 3)
                if t is not None:
                    act.wait_ge(s("w_ready"), t + 1)
                    act.activation(ffw[:, bass.ds(t, 1), :], w_ring[:, q:q + 1, :], ACT.Copy).then_inc(s("w_kept"), 1)
            run_tiles(act, None, slice_step, NT, 3)

            act.wait_ge(s("tok_turned"), 1)
            act.activation(tokT, ps[:, 4:6, :], ACT.Copy).then_inc(s("tokT_ready"), 1)
            act.activation(beta_row, ps[0:1, 6, :], ACT.Copy).then_inc(s("tokT_ready"), 1)
            act.wait_ge(s("stok_made"), 1)
            act.activation(stok, ps[0:HD, 0, :], ACT.Copy).then_inc(s("stok_ready"), 1)
            act.wait_ge(s("qkv_slices_made"), 1)
            for k, dst in enumerate((qT, kT, vv)):
                act.activation(dst, ps[0:HD, 1 + k, :], ACT.Copy).then_inc(s("qkv_slices_ready"), 1)
            act.wait_ge(s("scores_shifted"), 1)
            act.activation(attn, attn, ACT.Exp, scale=HD ** -0.5).then_inc(s("scores_exp"), 1)
            act.wait_ge(s("attn_turned"), 1)
            act.activation(attnT, ps[0:HD, 5, :], ACT.Copy).then_inc(s("attnT_ready"), 1)
            act.wait_ge(s("os_made"), 1)
            act.wait_ge(s("osT_zeroed"), 1)
            for hh in range(2):
                act.activation(osT[:, hh:H:2, hh * HD:(hh + 1) * HD],
                               ps[0:HD, 6, :].rearrange("p (h c) -> p h c", c=HD)[:, hh:H:2, :], ACT.Copy).then_inc(s("osT_ready"), 1)
            act.wait_ge(s("m_made"), 1)
            act.activation(m_out, ps[:, 0:4, 0:D], ACT.Copy).then_inc(s("m_ready"), 1)

            def out_step(i, par):
                t = live(i, 0)
                if t is not None:
                    if not isinstance(t, int) or t >= 2:
                        act.wait_ge(s("w_turned"), t - 1)
                    act.activation(wcopy_ring[:, par:par + 1, :], ffw[:, bass.ds(t, 1), :], ACT.Copy).then_inc(s("w_copied_back"), 1)
                t = live(i, 1)
                if t is not None:
                    par = 1 - par
                    act.wait_ge(s("w_turned"), t + 1)
                    if not isinstance(t, int) or t >= 2:
                        act.wait_ge(s("y_made"), t - 1)
                    act.activation(wT_ring[:, 4 * par:4 * par + 4, :], ps[:, par, 0:4 * PT].rearrange("p (k c) -> p k c", k=4), ACT.Copy).then_inc(s("wT_ready"), 1)
            run_tiles(act, None, out_step, NT, 1)

        @block.tensor
        def _(pe):
            pe.wait_ge(s("consts_set"), 1)
            pe.wait_ge(s("gw_loaded"), 64)
            for l in range(2):
                for k in range(2):
                    for b in range(2):
                        mm = pe.transpose(ps[:, 4 + l, k * D + b * P:k * D + (b + 1) * P],
                                          wstage[:, l, b, k * P:(k + 1) * P], ident[:, :])
                mm.then_inc(s("gw_turned"), 1)
            pe.wait_ge(s("wq_loaded"), 16)
            pe.wait_ge(s("small_loaded"), 14 * 16)
            for n in range(12):
                k, j = divmod(n, 6)
                taps = wq_stage[:, j, :].rearrange("p (c f) -> p c f", f=5)
                mm = pe.transpose(ps[:, n // 4, n % 4 * P:(n % 4 + 1) * P], taps[:, k * P:(k + 1) * P, 2], ident[:, :])
                if n % 4 == 3:
                    mm.then_inc(s("mw_turned"), 1)
            for n in range(8):
                k, b = divmod(n, 2)
                if n == 4:
                    pe.wait_ge(s("gw_ready"), 4)
                mm = pe.transpose(ps[:, 3 + n // 4, n % 4 * P:(n % 4 + 1) * P], wres_stage[:, b, k * P:(k + 1) * P], ident[:, :])
                if n % 4 == 3:
                    mm.then_inc(s("mw_turned"), 1)
            pe.wait_ge(s("counts_ready"), 1)
            pe.matmul(ps[:, 7, 0:NT], triu[:, :], counts[:, :], start=True, stop=True)
            pe.matmul(ps[:, 7, 64:64 + NT], ones[:, :], counts[:, :], start=True, stop=True).then_inc(s("totals_made"), 1)
            pe.wait_ge(s("ends_ready"), 1)
            pe.transpose(ps[0:NT, 6, 0:P], bins[:, 1, :], ident[:, :]).then_inc(s("ends_turned"), 1)
            pe.wait_ge(s("tcmp_ready"), 1)
            half = NCH // 2
            for k in range(2):
                mm = pe.matmul(ps[0:1, 6 + k, 0:half], ones[0:NT, 0:1], tcmp[:, k * half:(k + 1) * half], start=True, stop=True)
            mm.then_inc(s("tiles_made"), 1)

            pe.wait_ge(s("mw_ready"), 5)
            def mean_step(i, par):
                t = live(i, 1)
                if t is not None:
                    pe.wait_ge(s("scaled"), t + 1)
                    pe.matmul(ps[:, 0, 0:D], ones[0:PT, :], hin[:, 1 - par, :], start=isinstance(t, int) and t == 0,
                              stop=isinstance(t, int) and t == NT - 1).then_inc(s("scaled_used"), 1)
            run_tiles(pe, None, mean_step, NT, 1)
            pe.wait_ge(s("scaled_used"), NT)
            pe.sem_inc(s("means_summed"), 1)
            pe.wait_ge(s("mu_ready"), 1)
            for k in range(2):
                mm = pe.transpose(ps[:, 3, k * P:(k + 1) * P], mu[:, k * P:(k + 1) * P], ident[:, :])
            mm.then_inc(s("mu_turned"), 1)

            def gram_step(i, par):
                t = live(i, 1)
                if t is not None:
                    q = 1 - par
                    pe.wait_ge(s("centred"), t + 1)
                    first, last = isinstance(t, int) and t == 0, isinstance(t, int) and t == NT - 1
                    for k in range(2):
                        mm = pe.matmul(ps[:, 1 + k, 0:D], hin[:, q, k * P:(k + 1) * P], hin[:, q, :], start=first, stop=last)
                    mm.then_inc(s("centred_used"), 1)
            run_tiles(pe, None, gram_step, NT, 1)
            pe.wait_ge(s("centred_used"), NT)
            pe.sem_inc(s("gram_made"), 1)
            pe.wait_ge(s("cov_ready"), 1)
            pe.wait_ge(s("tiles_kept"), 1)
            for m in range(2):
                for n in range(2):
                    for k in range(2):
                        mm = pe.matmul(ps[:, 4 + 2 * m + n, 0:CH3 // 2], cov[:, k, m * P:(m + 1) * P],
                                       wqkv[:, k, n * CH3 // 2:(n + 1) * CH3 // 2], start=(k == 0), stop=(k == 1))
            mm.then_inc(s("cw_made"), 1)
            pe.wait_ge(s("prods_ready"), 1)
            for w in range(2):
                for n in range(2):
                    for k in range(2):
                        mm = pe.matmul(ps[:, 2 * w + n, 0:CH3 // 2], ones[:, :], prod[:, 2 * w + k, n * CH3 // 2:(n + 1) * CH3 // 2],
                                       start=(k == 0), stop=(k == 1))
            mm.then_inc(s("bnsums_made"), 1)

            pe.wait_ge(s("mixw_ready"), 1)

            def mix_step(i, par):
                q = 1 - par
                t = live(i, 0)
                if t is not None:
                    pe.wait_ge(s("hin_ready"), t + 1)
                    if not isinstance(t, int) or t >= 4:
                        pe.wait_ge(s("ft_out"), t - 3)
                    if not (isinstance(t, int) and t == 0):
                        pe.wait_ge(s("hT_ready"), t)
                    for k in range(2):
                        mm = pe.transpose(ps[:, 6, k * PT:(k + 1) * PT], hin[:, par, k * P:(k + 1) * P], ident[0:PT, 0:PT])
                    mm.then_inc(s("hin_turned"), 1)
                t = live(i, 1)
                if t is not None:
                    pe.wait_ge(s("relu_done"), t + 1)
                    if not (isinstance(t, int) and t == 0):
                        pe.wait_ge(s("rT_ready"), t)
                    for j in range(6):
                        mm = pe.transpose(ps[:, 4 + j // 3, j % 3 * PT:(j % 3 + 1) * PT], cat[:, q, j * P:(j + 1) * P], ident[0:PT, 0:PT])
                    mm.then_inc(s("r_turned"), 1)
                t = live(i, 3)
                if t is not None:
                    pe.wait_ge(s("o_ready"), t + 1)
                    if not (isinstance(t, int) and t == 0):
                        pe.wait_ge(s("oT_ready"), t)
                    for j in range(4):
                        mm = pe.transpose(ps[:, 7, j * PT:(j + 1) * PT], o_ring[:, q, j * P:(j + 1) * P], ident[0:PT, 0:PT])
                    mm.then_inc(s("o_turned"), 1)
                t = live(i, 1)
                if t is not None:
                    pe.wait_ge(s("rT_ready"), t + 1)
                    if not (isinstance(t, int) and t == 0):
                        pe.wait_ge(s("s_kept"), t)
                    for j in range(6):
                        mm = pe.matmul(ps[0:PT, 2 + j // 3, j % 3 * P:(j % 3 + 1) * P], rT_ring[:, q, j, :], wblock[:, j, :], start=True, stop=True)
                    mm.then_inc(s("s_made"), 1)
                t = live(i, 0)
                if t is not None:
                    pe.wait_ge(s("hT_ready"), t + 1)
                    if not (isinstance(t, int) and t == 0):
                        pe.wait_ge(s("relu_done"), t)
                    for n in range(2):
                        cs = slice(n * CH3 // 2, (n + 1) * CH3 // 2)
                        pe.matmul(ps[0:PT, n, 0:CH3 // 2], ones3[:, 0:PT], qbias3[:, cs], start=True, stop=False)
                        for k in range(2):
                            mm = pe.matmul(ps[0:PT, n, 0:CH3 // 2], hT_ring[:, 2 * par + k, :], wqkv[:, k, cs], start=False, stop=(k == 1))
                    mm.then_inc(s("qkv_made"), 1)
                t = live(i, 3)
                if t is not None:
                    pe.wait_ge(s("oT_ready"), t + 1)
                    for j in range(4):
                        mm = pe.matmul(ps[0:PT, 6, D:2 * D], oT_ring[:, 4 * q + j, :], wres[:, j, :], start=(j == 0), stop=(j == 3))
                    mm.then_inc(s("ft_made"), 1)
            run_tiles(pe, None, mix_step, NT, 3)

            for l in range(2):
                pe.wait_ge(s("agg_added_credit"), 1)

                def group(j, half, l=l):
                    pe.wait_ge(s("onehot_ready"), (j * 2 + half) + (NGRP * l + 1))
                    pe.wait_ge(s(f"gathered{half}"), (j + (NGRP // 2 * l + 1)) * (16 * GRP))
                    for k in range(GRP):
                        n = (j * 2 + half) * GRP + (k + NCH * l)
                        if not (isinstance(n, int) and n < 4):
                            pe.wait_ge(s("agg_added"), n - 3)
                        pe.matmul(ps[0:PT, k % 4, 0:257], onehot[:, GRP * half + k, :], gat[:, GRP * half + k, :],
                                  start=True, stop=True).then_inc(s("agg_made"), 1)
                for half in range(2):
                    group(0, half)
                with pe.Fori(1, NGRP // 2) as j:
                    for half in range(2):
                        group(j, half)

                def post_step(i, par, l=l):
                    t = live(i, 0)
                    if t is not None:
                        pe.wait_ge(s("u_ready"), t + (NT * l + 1))
                        if not isinstance(t, int) or t >= 2:
                            pe.wait_ge(s("uT_ready"), t + (NT * l - 1))
                        for k in range(2):
                            mm = pe.transpose(ps[:, 4 + par, k * P:k * P + PT], u_ring[:, par, k * P:(k + 1) * P], ident[0:PT, 0:PT])
                        mm.then_inc(s("u_turned"), 1)
                    t = live(i, 1)
                    if t is not None:
                        q = 1 - par
                        pe.wait_ge(s("uT_ready"), t + (NT * l + 1))
                        if not isinstance(t, int) or t >= 2:
                            pe.wait_ge(s("h_kept"), t + (NT * l - 1))
                        pe.matmul(ps[0:PT, 6 + q, 0:D], ones3[:, 0:PT], gbias3[l][:, :], start=True, stop=False)
                        for k in range(2):
                            mm = pe.matmul(ps[0:PT, 6 + q, 0:D], uT_ring[:, 2 * q + k, :], wT[l][:, k, :],
                                           start=False, stop=(k == 1))
                        mm.then_inc(s("h_made"), 1)
                pe.wait_ge(s("gw_ready"), 4)
                pe.wait_ge(s("gbias_ready"), 2)
                run_tiles(pe, None, post_step, NT, 1)

            pe.wait_ge(s("ffn_loaded"), 64)
            for n in range(8):
                j, k = divmod(n, 2)
                mm = pe.transpose(ps[:, n // 4, n % 4 * P:(n % 4 + 1) * P], wx_stage[:, k, j * P:(j + 1) * P], ident[:, :])
                if n % 4 == 3:
                    mm.then_inc(s("wx_turned"), 1)
            pe.transpose(ps[0:HD, 2, 0:H], b_x8[:, :], ident[0:H, 0:H]).then_inc(s("bx_turned"), 1)
            pe.wait_ge(s("wxT_ready"), 2)
            for k in range(2):
                for h in range(H):
                    r0 = h % 2 * HD
                    mm = pe.matmul(ps[:, 4 + 2 * (h % 2) + k, h * G:(h + 1) * G], wxT[r0:r0 + HD, h // 2, k * P:(k + 1) * P],
                                   w_small[r0:r0 + HD, 0, :], start=True, stop=True)
            mm.then_inc(s("wc_made"), 1)
            pe.wait_ge(s("bxT_ready"), 1)
            for h in range(H):
                mm = pe.matmul(ps[0:3, 3, h * G:(h + 1) * G], b_x8T[:, h:h + 1].to_broadcast([HD, 3]), w_small[0:HD, 0, :], start=True, stop=True)
            mm.then_inc(s("lb_made"), 1)

            pe.wait_ge(s("wc_ready"), 1)

            def slice_step(i, par):
                t = live(i, 1)
                if t is not None:
                    q = 1 - par
                    pe.wait_ge(s("xlT_ready"), t + 1)
                    if not isinstance(t, int) or t >= 2:
                        pe.wait_ge(s("shifted"), t - 1)
                    pe.matmul(ps[0:PT, 4 + q, :], ones3[:, 0:PT], lbias3[:, :], start=True, stop=False)
                    for k in range(2):
                        mm = pe.matmul(ps[0:PT, 4 + q, :], xlT_ring[:, 2 * q + k, :], wc[:, k, :], start=False, stop=(k == 1))
                    mm.then_inc(s("logits_made"), 1)
                t = live(i, 0)
                if t is not None:
                    pe.wait_ge(s("xl_ready"), t + 1)
                    if not isinstance(t, int) or t >= 2:
                        pe.wait_ge(s("xlT_ready"), t - 1)
                    for k in range(2):
                        mm = pe.transpose(ps[:, 6 + par, k * PT:(k + 1) * PT], xl_ring[:, par, k * P:(k + 1) * P], ident[0:PT, 0:PT])
                    mm.then_inc(s("xl_turned"), 1)
                t = live(i, 3)
                if t is not None:
                    pe.wait_ge(s("w_ready"), t + 1)
                    pe.wait_ge(s("xl_copied"), t + 1)
                    first, last = isinstance(t, int) and t == 0, isinstance(t, int) and t == NT - 1
                    for j in range(4):
                        w = w_ring[:, 1 - par, j * P:(j + 1) * P]
                        pe.matmul(ps[:, j, 0:D], w, nodes[:, bass.ds(t, 1), :].squeeze(), start=first, stop=last, skip_group_check=True)
                        mm = pe.matmul(ps[:, j, D:D + 1], w, ones[0:PT, 0:1], start=False, stop=last, skip_group_check=True)
                    mm.then_inc(s("w_used"), 1)
            run_tiles(pe, None, slice_step, NT, 3)
            pe.wait_ge(s("w_used"), NT)
            pe.sem_inc(s("slices_summed"), 1)

            pe.wait_ge(s("tok_ready"), 1)
            for k in range(2):
                for j in range(4):
                    pe.transpose(ps[:, 4 + k, j * P:(j + 1) * P], tok[:, j, k * P:(k + 1) * P], ident[:, :])
            for j in range(4):
                mm = pe.transpose(ps[0:1, 6, j * P:(j + 1) * P], tok[:, j, D:D + 1], ident[:, :])
            mm.then_inc(s("tok_turned"), 1)
            pe.wait_ge(s("tokT_ready"), 2)
            for h in range(H):
                hs = slice(h * HD, (h + 1) * HD)
                for k in range(2):
                    pe.matmul(ps[0:HD, 0, hs], w_fx[:, k, hs], tokT[:, k, hs], start=(k == 0), stop=False)
                mm = pe.matmul(ps[0:HD, 0, hs], b_fx[:, hs], beta_row[:, hs], start=False, stop=True)
            mm.then_inc(s("stok_made"), 1)
            pe.wait_ge(s("stok_ready"), 1)
            pe.matmul(ps[0:HD, 1, :], w_small[0:HD, 1, :], stok, start=True, stop=True)
            pe.matmul(ps[0:HD, 2, :], w_small[0:HD, 2, :], stok, start=True, stop=True)
            for h in range(H):
                hs = slice(h * HD, (h + 1) * HD)
                mm = pe.matmul(ps[0:HD, 3, hs], stok[:, hs], w_small[0:HD, 3, :], start=True, stop=True)
            mm.then_inc(s("qkv_slices_made"), 1)
            pe.wait_ge(s("qkv_slices_ready"), 3)
            for h in range(H):
                hs = slice(h * HD, (h + 1) * HD)
                mm = pe.matmul(ps[0:HD, 4, hs], qT[:, hs], kT[:, hs], start=True, stop=True)
            mm.then_inc(s("scores_made"), 1)
            pe.wait_ge(s("attn_ready"), 1)
            for h in range(H):
                hs = slice(h * HD, (h + 1) * HD)
                mm = pe.transpose(ps[0:HD, 5, hs], attn[:, hs], ident[0:HD, 0:HD])
            mm.then_inc(s("attn_turned"), 1)
            pe.wait_ge(s("attnT_ready"), 1)
            for h in range(H):
                hs = slice(h * HD, (h + 1) * HD)
                mm = pe.matmul(ps[0:HD, 6, hs], vv[:, hs], attnT[:, hs], start=True, stop=True)
            mm.then_inc(s("os_made"), 1)
            pe.wait_ge(s("osT_ready"), 2)
            for h in range(H):
                mm = pe.matmul(ps[:, h // 2, 0:D], osT[:, h, :], w_out[:, h, :], start=(h % 2 == 0), stop=(h % 2 == 1))
            mm.then_inc(s("m_made"), 1)

            pe.wait_ge(s("m_ready"), 1)

            def out_step(i, par):
                t = live(i, 0)
                if t is not None:
                    pe.wait_ge(s("w_copied_back"), t + 1)
                    if not isinstance(t, int) or t >= 2:
                        pe.wait_ge(s("wT_ready"), t - 1)
                    for j in range(4):
                        mm = pe.transpose(ps[:, par, j * PT:(j + 1) * PT], wcopy_ring[:, par, j * P:(j + 1) * P], ident[0:PT, 0:PT])
                    mm.then_inc(s("w_turned"), 1)
                t = live(i, 1)
                if t is not None:
                    q = 1 - par
                    pe.wait_ge(s("wT_ready"), t + 1)
                    if not isinstance(t, int) or t >= 2:
                        pe.wait_ge(s("out_ready"), t - 1)
                    pe.matmul(ps[0:PT, 4 + q, 0:D], ones3[:, 0:PT], gbias3[0][:, :], start=True, stop=False)
                    for j in range(4):
                        mm = pe.matmul(ps[0:PT, 4 + q, 0:D], wT_ring[:, 4 * q + j, :], m_out[:, j, :], start=False, stop=(j == 3))
                    mm.then_inc(s("y_made"), 1)
            run_tiles(pe, None, out_step, NT, 1)

        @block.vector
        def _(dve):
            do = Order(dve, s("dve_order"))
            link = do.link

            dve.wait_ge(s("edges_loaded"), 64)
            dve.wait_ge(s("bin_id_set"), 1)
            link(dve.tensor_scalar(quot, e_src, 1.0 / NT, -0.49, ALU.mult, ALU.add))
            link(dve.scalar_tensor_tensor(out=bin16, in0=quot, scalar=-float(NT), in1=e_src, op0=ALU.mult, op1=ALU.add))
            link(dve.scalar_tensor_tensor(out=code, in0=quot, scalar=8192.0, in1=code, op0=ALU.mult, op1=ALU.add))
            with dve.Fori(0, NT // UNR) as g:
                do.turn()
                do.link_all(dve.tensor_scalar(spare16[k], bin16, bin_id[:, bass.ds(g * UNR + k, 1)], None, ALU.is_equal, ALU.add,
                                              accum_out=counts[:, bass.ds(g * UNR + k, 1)]) for k in range(UNR))
            dve.engine_nop().then_inc(s("counts_ready"), 1)
            dve.wait_ge(s("totals_made"), 1)
            link(dve.tensor_scalar(bins_i[:, :], ps[:, 7, 64:64 + NT], float(P - 1), None, ALU.add))
            link(dve.tensor_scalar(bins_i[:, :], bins_i[:, :], 7, None, ALU.arith_shift_right))
            link(dve.tensor_scalar(bins[:, 0, :], bins_i[:, :], float(P), None, ALU.mult))
            link(dve.tensor_tensor_scan(bins[:, 1, :], bins[:, 0, :], ones[:, 0:NT], 0.0, ALU.add, ALU.mult))
            dve.engine_nop().then_inc(s("ends_ready"), 1)
            link(dve.tensor_tensor(bins[:, 2, :], bins[:, 1, :], bins[:, 0, :], ALU.subtract))
            link(dve.scalar_tensor_tensor(out=carry[:, :], in0=ps[:, 7, 0:NT], scalar=-1.0, in1=bins[:, 2, :], op0=ALU.add, op1=ALU.add))
            for c0, c1 in ((0, PIECE1 * STG), (PIECE1 * STG, EC)):
                n = c1 - c0
                side = UNR if UNR * n <= EC else 1
                at = [slice(k * n, (k + 1) * n) for k in range(side)]
                with dve.Fori(0, NT // side) as g:
                    do.turn()
                    do.link_all(dve.tensor_scalar(mask16[:, at[k]], bin16[:, c0:c1], bin_id[:, bass.ds(g * side + k, 1)], None, ALU.is_equal)
                                for k in range(side))
                    do.link_all(dve.tensor_tensor_scan(count_run[:, at[k]], mask16[:, at[k]], ones[:, 0:1].to_broadcast([P, n]),
                                                       carry[:, bass.ds(g * side + k, 1)], ALU.add, ALU.mult) for k in range(side))
                    dve.nop(nofuse=True)
                    for k in range(side):
                        link(dve.copy_predicated(pos_f[:, c0:c1], mask16[:, at[k]], count_run[:, at[k]]))
                    do.link_all(dve.tensor_scalar(carry[:, bass.ds(g * side + k, 1)], count_run[:, (k + 1) * n - 1:(k + 1) * n], 1.0, None, ALU.mult)
                                for k in range(side))
                link(dve.tensor_copy(pos_i[:, c0:c1], pos_f[:, c0:c1]))
                link(dve.tensor_scalar(quot[:, c0:c1], pos_i[:, c0:c1], 7, None, ALU.arith_shift_right))
                link(dve.tensor_scalar(pos_i[:, c0:c1], pos_i[:, c0:c1], P - 1, None, ALU.bitwise_and))
                dve.scalar_tensor_tensor(out=pos_i[:, c0:c1], in0=pos_i[:, c0:c1], scalar=float(NCH), in1=quot[:, c0:c1],
                                         op0=ALU.mult, op1=ALU.add).then_inc(s("positions"), 1)
                dve.wait_ge(s("positions"), 1 if c0 == 0 else 2)

            dve.wait_ge(s("ends_turned"), 1)
            link(dve.tensor_scalar(chunk_end[:, :], ps[0:NT, 6, 0:1], 1.0 / P, None, ALU.mult))
            dve.tensor_scalar(tcmp, tcmp, chunk_end[:, 0:1], None, ALU.is_ge).then_inc(s("tcmp_ready"), 1)
            dve.wait_ge(s("tiles_made"), 1)
            link(dve.tensor_scalar(tile_row.rearrange("p (k c) -> p k c", k=2), ps[0:1, 6:8, 0:NCH // 2], float(NT - 1), None, ALU.min))
            dve.sem_inc(s("tiles_kept"), 1)

            def split3(dst, src, n):
                part = [split_bf[:, k, 0:n] for k in range(3)]
                link(dve.tensor_copy(part[0], src))
                link(dve.tensor_tensor(split[:, 0, 0:n], src, part[0], ALU.subtract))
                link(dve.tensor_copy(part[1], split[:, 0, 0:n]))
                link(dve.tensor_tensor(split[:, 1, 0:n], split[:, 0, 0:n], part[1], ALU.subtract))
                link(dve.tensor_copy(part[2], split[:, 1, 0:n]))
                link(dve.tensor_scalar(split[:, 2, 0:n], part[0], ident[0:3, 0:1], None, ALU.mult))
                link(dve.scalar_tensor_tensor(out=split[:, 3, 0:n], in0=part[1], scalar=ident[0:3, 1:2], in1=split[:, 2, 0:n], op0=ALU.mult, op1=ALU.add))
                link(dve.scalar_tensor_tensor(out=dst, in0=part[2], scalar=ident[0:3, 2:3], in1=split[:, 3, 0:n], op0=ALU.mult, op1=ALU.add))
            dve.wait_ge(s("consts_set"), 1)
            dve.wait_ge(s("gw_loaded"), 64)
            for l in range(2):
                split3(gbias3[l][:, :], brow[:, l, :], D)
                dve.engine_nop().then_inc(s("gbias_ready"), 1)

            dve.wait_ge(s("small_loaded"), 14 * 16)
            link(dve.memset(wblock, 0.0))
            for j in range(6):
                link(dve.transpose(pw_turned[:, j, :], pw_stage[:, j, :]))
            for g in range(4):
                r = slice(32 * g, 32 * g + 32)
                link(dve.tensor_tensor(wblock[r, :, r], pw_turned[r, :, :], dw_stage[r, :, 2:3].to_broadcast([32, 6, 32]), ALU.mult))

            def mean_var(ready):
                mean_e, m2_e, mean_o, m2_o = (lnst[:, :, k] for k in (1, 2, 4, 5))
                link(dve.tensor_tensor(cols[:, 0, :], mean_e, mean_o, ALU.add))
                link(dve.tensor_scalar(mean[:, :], cols[:, 0, :], 0.5, None, ALU.mult))
                link(dve.tensor_tensor(cols[:, 1, :], mean_e, mean_o, ALU.subtract))
                link(dve.scalar_tensor_tensor(out=cols[:, 2, :], in0=cols[:, 1, :], scalar=0.25, in1=cols[:, 1, :], op0=ALU.mult, op1=ALU.mult))
                link(dve.tensor_tensor(cols[:, 3, :], m2_e, m2_o, ALU.add))
                link(dve.scalar_tensor_tensor(out=cols[:, 1, :], in0=cols[:, 3, :], scalar=1.0 / D, in1=cols[:, 2, :], op0=ALU.mult, op1=ALU.add))
                dve.tensor_scalar(cols[:, 0, :], cols[:, 1, :], LN_EPS, None, ALU.add).then_inc(s(ready), 1)
            dve.wait_ge(s("x_loaded"), 80)
            with dve.Fori(0, NT // UNR) as g:
                do.turn()
                do.link_all(dve.bn_stats(lnst[:, bass.ds(t, 1), :], nodes[:, bass.ds(t, 1), :]) for t in (g * UNR + k for k in range(UNR)))
            mean_var("xvar_ready")
            dve.wait_ge(s("xstd_ready"), 1)
            link(dve.reciprocal(cols[:, 2, :], cols[:, 1, :]))
            with dve.Fori(0, NT // UNR) as g:
                do.turn()
                do.link_all(dve.tensor_scalar(nodes[:, bass.ds(t, 1), :], nodes[:, bass.ds(t, 1), :], mean[:, bass.ds(t, 1)],
                                              cols[:, 2, bass.ds(t, 1)], ALU.subtract, ALU.mult) for t in (g * UNR + k for k in range(UNR)))
            dve.engine_nop().then_inc(s("xn_ready"), 1)

            c0, c1, c2, c3 = (cols[:, k, :] for k in range(4))
            link(dve.tensor_tensor(c3, c2, c2, ALU.mult))
            link(dve.scalar_tensor_tensor(out=c2, in0=c0, scalar=-LN_EPS, in1=c3, op0=ALU.add, op1=ALU.mult))
            dve.tensor_scalar(c0, c2, float(D), 1e-30, ALU.mult, ALU.max).then_inc(s("xnorm2_ready"), 1)
            dve.wait_ge(s("xnorm_ready"), 1)
            link(dve.tensor_scalar(c2, c1, MAXN, None, ALU.min))
            link(dve.tensor_scalar(c0, c2, 1.0, None, ALU.add))
            dve.tensor_scalar(c3, c2, -1.0, 1.0, ALU.mult, ALU.add).then_inc(s("log_args"), 1)
            dve.wait_ge(s("logs_ready"), 2)
            link(dve.tensor_tensor(c0, c0, c3, ALU.subtract))
            link(dve.tensor_scalar(fac[:, :], c0, 0.5, None, ALU.mult))
            link(dve.tensor_tensor(c3, c2, c2, ALU.mult))
            link(dve.tensor_scalar(c0, c3, 1.0 / 13, 1.0 / 11, ALU.mult, ALU.add))
            for k in (9, 7, 5, 3, 1):
                link(dve.tensor_tensor(c0, c0, c3, ALU.mult))
                link(dve.tensor_scalar(c0, c0, 1.0 / k, None, ALU.add))
            link(dve.tensor_tensor(c0, c0, c2, ALU.mult))
            link(dve.tensor_scalar(few[:, :], c2, 0.2, None, ALU.is_lt))
            link(dve.copy_predicated(fac[:, :], few[:, :], c0))
            link(dve.reciprocal(c3, c1))
            link(dve.tensor_tensor(fac[:, :], fac[:, :], c3, ALU.mult))
            def scale_step(i, par):
                t = live(i, 0)
                if t is not None:
                    if not isinstance(t, int) or t >= 2:
                        dve.wait_ge(s("scaled_used"), t - 1)
                    dve.tensor_scalar(hin[:, par:par + 1, :], nodes[:, bass.ds(t, 1), :], fac[:, bass.ds(t, 1)], None, ALU.mult).then_inc(s("scaled"), 1)
            run_tiles(dve, None, scale_step, NT, 0)
            dve.wait_ge(s("mu_ready"), 1)

            def centre_step(i, par):
                t = live(i, 0)
                if t is not None:
                    if not isinstance(t, int) or t >= 2:
                        dve.wait_ge(s("centred_used"), t - 1)
                    dve.scalar_tensor_tensor(out=hin[:, par:par + 1, :], in0=nodes[:, bass.ds(t, 1), :], scalar=fac[:, bass.ds(t, 1)],
                                             in1=mu[0:PT, :].unsqueeze(1), op0=ALU.mult, op1=ALU.subtract).then_inc(s("centred"), 1)
            run_tiles(dve, None, centre_step, NT, 0)
            dve.wait_ge(s("muT_ready"), 1)
            for k in range(2):
                link(dve.tensor_scalar(prod[:, 2 + k, :], wqkv[:, k, :], muT[:, k:k + 1], None, ALU.mult))
            dve.wait_ge(s("cw_made"), 1)
            for k in range(2):
                link(dve.tensor_tensor(prod[:, k, :].rearrange("p (a b) -> p a b", a=2), ps[:, 4 + 2 * k:6 + 2 * k, 0:CH3 // 2],
                                       wqkv[:, k, :].rearrange("p (a b) -> p a b", a=2), ALU.mult))
            dve.sem_inc(s("prods_ready"), 1)
            dve.wait_ge(s("bnsums_made"), 1)
            halves = lambda ap: ap.rearrange("p (a b) -> p a b", a=2)
            link(dve.tensor_scalar(halves(prod[:, 2, :]), ps[:, 2:4, 0:CH3 // 2], 1.0, None, ALU.mult))
            dve.tensor_scalar(halves(prod[:, 0, :]), ps[:, 0:2, 0:CH3 // 2], LN_EPS, None, ALU.add).then_inc(s("bnvar_ready"), 1)
            dve.wait_ge(s("bnstd_ready"), 1)
            link(dve.reciprocal(prod[:, 3, :], prod[:, 1, :]))
            link(dve.tensor_tensor(prod[:, 3, :], prod[:, 3, :], bn_gam, ALU.mult))
            link(dve.tensor_tensor(prod[:, 2, :], prod[:, 2, :], prod[:, 3, :], ALU.mult))
            link(dve.tensor_tensor(prod[:, 2, :], bn_bet, prod[:, 2, :], ALU.subtract))
            for k in range(2):
                link(dve.tensor_tensor(wqkv[:, k, :], wqkv[:, k, :], prod[:, 3, :], ALU.mult))
            split3(qbias3, prod[0:3, 2, :], CH3)
            dve.sem_inc(s("mixw_ready"), 1)

            def mix_step(i, par):
                q = 1 - par
                t = live(i, 0)
                if t is not None:
                    if not isinstance(t, int) or t >= 2:
                        dve.wait_ge(s("hin_turned"), t - 1)
                    dve.tensor_scalar(hin[:, par:par + 1, :], nodes[:, bass.ds(t, 1), :], fac[:, bass.ds(t, 1)], None, ALU.mult).then_inc(s("hin_ready"), 1)
                t, before = live(i, 2), live(i, 4)
                c = lambda k: sm[:, par, k:k + 1]
                if t is not None:
                    dve.wait_ge(s("norms2_ready"), t + 1)
                    link(dve.tensor_scalar(c(5), c(0), 1e-30, None, ALU.max))
                    dve.tensor_tensor(c(6), c(5), c(1), ALU.add).then_inc(s("norms2_clipped"), 1)
                if before is not None:
                    dve.wait_ge(s("on2_ready"), before + 1)
                    dve.tensor_scalar(c(15), c(3), 1e-30, None, ALU.max).then_inc(s("on2_clipped"), 1)
                    link(dve.tensor_tensor(c(4), c(12), c(12), ALU.mult))
                if t is not None:
                    part = cat[:, par, :].rearrange("p (g c) -> p g c", c=96)
                    e = [ev[:, k, :].rearrange("p (g c) -> p g c", c=32) for k in range(4)]
                    link(dve.tensor_scalar(e[0], part[:, :, 32:64], 0.0, None, ALU.max))
                    link(dve.tensor_reduce(ev[:, 1, 0:NG], e[0], AX.X, ALU.add))
                    link(dve.scalar_tensor_tensor(out=e[2], in0=part[:, :, 0:32], scalar=0.0,
                                                  in1=ev[:, 1, 0:NG].unsqueeze(2).to_broadcast([PT, NG, 32]), op0=ALU.max, op1=ALU.mult))
                    link(dve.tensor_tensor(e[3], part[:, :, 64:96], e[2], ALU.mult))
                if t is not None:
                    dve.wait_ge(s("norms_ready"), t + 1)
                if before is not None:
                    dve.wait_ge(s("on_ready"), before + 1)
                if t is not None:
                    do.mark(dve.reciprocal(c(7), c(5)))
                if before is not None:
                    do.mark(dve.tensor_scalar(c(16), c(15), c(4), 1e-15, ALU.mult, ALU.max))
                do.wait()
                if t is not None:
                    do.mark(dve.tensor_scalar(c(8), c(5), ATANH_MAXN, c(7), ALU.min, ALU.mult))
                if before is not None:
                    do.mark(dve.reciprocal(c(17), c(16)))
                do.wait()
                if t is not None:
                    do.mark(dve.tensor_scalar(c(9), c(6), c(8), 1e-15, ALU.mult, ALU.max))
                if before is not None:
                    do.mark(dve.tensor_scalar(c(18), c(16), ATANH_MAXN, c(17), ALU.min, ALU.mult))
                do.wait()
                if t is not None:
                    do.mark(dve.reciprocal(c(10), c(9)))
                if before is not None:
                    do.mark(dve.tensor_tensor(c(19), c(18), c(4), ALU.mult))
                do.wait()
                if t is not None:
                    link(dve.tensor_scalar(c(11), c(9), ATANH_MAXN, c(10), ALU.min, ALU.mult))
                    link(dve.tensor_tensor(c(12), c(11), c(8), ALU.mult))
                if t is not None:
                    link(dve.tensor_scalar(e[0], part[:, :, 64:96], c(12), 1e-15, ALU.mult, ALU.add))
                    link(dve.reciprocal(ev[:, 1, :], ev[:, 0, :]))
                    if not isinstance(t, int) or t >= 2:
                        dve.wait_ge(s("o_turned"), t - 1)
                        dve.wait_ge(s("on2_ready"), t - 1)
                    dve.scalar_tensor_tensor(out=o_ring[:, par, :], in0=ev[:, 3, :], scalar=c(12), in1=ev[:, 1, :],
                                             op0=ALU.mult, op1=ALU.mult).then_inc(s("o_ready"), 1)
                t = live(i, 5)
                if t is not None:
                    mt = mixo[:, bass.ds(t, 1), :]
                    dve.wait_ge(s("ft_out"), t + 1)
                    dve.scalar_tensor_tensor(out=mt, in0=mt, scalar=sm[:, 1 - par, 19:20],
                                             in1=bres.unsqueeze(1), op0=ALU.mult, op1=ALU.add).then_inc(s("ft_kept"), 1)
            run_tiles(dve, do, mix_step, NT, 5)
            dve.wait_ge(s("mix_tiles_done"), 1)
            dve.tensor_scalar(c0, nf2[:, :], 1e-30, None, ALU.max).then_inc(s("fnorm2_ready"), 1)
            dve.wait_ge(s("ftanh_ready"), 1)
            link(dve.tensor_scalar(c2, c2, MAXN, None, ALU.min))
            link(dve.reciprocal(c3, c1))
            link(dve.tensor_tensor(nf2[:, :], c2, c3, ALU.mult))

            dve.wait_ge(s("sorted_loaded"), 16)
            link(dve.tensor_scalar(s_dst, s_code, 8191, None, ALU.bitwise_and))
            link(dve.tensor_scalar(s_code, s_code, 13, None, ALU.arith_shift_right))
            dve.tensor_scalar(s_row, s_code, -1.0, None, ALU.mult).then_inc(s("sorted_split"), 1)

            for l in range(2):
                link(dve.memset(acc[:, :, :], 0.0))
                link(dve.memset(gat[:, :, D:257], 1.0))
                dve.engine_nop().then_inc(s("ring_free"), 1)
                dve.engine_nop().then_inc(s("agg_added_credit"), 1)

                def add_groups(j, l=l):
                    _, tiles = nc.values_load_multi_w_load_instructions(
                        tile_row[0:1, bass.ds(j * (2 * GRP), 2 * GRP)], [mybir.EngineType.DVE], min_val=0, max_val=NT - 1)
                    for k in range(2 * GRP):
                        n = j * (2 * GRP) + (k + NCH * l)
                        dve.wait_ge(s("agg_made"), n + 1)
                        if not (isinstance(n, int) and n == 0):
                            dve.wait_ge(s("agg_added"), n)
                        at = acc[:, bass.ds(tiles[k], 1), :]
                        dve.tensor_tensor(at, ps[0:PT, k % 4, 0:257].unsqueeze(1), at, ALU.add).then_inc(s("agg_added"), 1)

                add_groups(0)
                if l == 0:
                    with dve.Fori(1, NT + 1) as j:
                        dve.wait_ge(s("x_tile_loaded"), j * 16)
                        mt = mixo[:, bass.ds(j - 1, 1), :]
                        dve.scalar_tensor_tensor(out=mt, in0=mt, scalar=nf2[:, bass.ds(j - 1, 1)], in1=x_tile.unsqueeze(1),
                                                 op0=ALU.mult, op1=ALU.add).then_inc(s("x_tile_used"), 1)
                        add_groups(j)
                    for j in range(NT + 1, NGRP // 2):
                        add_groups(j)
                else:
                    with dve.Fori(1, NGRP // 2) as j:
                        add_groups(j)
                dve.wait_ge(s("agg_added"), NCH * (l + 1))

                link(dve.tensor_scalar(cols[:, 3, :], acc[:, :, D], 1.0, None, ALU.max))
                link(dve.reciprocal(cols[:, 2, :], cols[:, 3, :]))

                def post_step(i, par, l=l):
                    t = live(i, 0)
                    if t is not None:
                        if not isinstance(t, int) or t >= 2:
                            dve.wait_ge(s("u_turned"), t + (NT * l - 1))
                        dve.scalar_tensor_tensor(out=u_ring[:, par:par + 1, :], in0=acc[:, bass.ds(t, 1), 0:D],
                                                 scalar=cols[:, 2, bass.ds(t, 1)], in1=nodes[:, bass.ds(t, 1), :],
                                                 op0=ALU.mult, op1=ALU.add).then_inc(s("u_ready"), 1)
                    t = live(i, 4)
                    if t is not None:
                        dve.wait_ge(s("h_kept"), t + (NT * l + 1))
                        dve.bn_stats(lnst[:, bass.ds(t, 1), :], acc[:, bass.ds(t, 1), 0:D]).then_inc(s("h_stats"), 1)
                run_tiles(dve, None, post_step, NT, 4)
                dve.wait_ge(s("h_stats"), NT * (l + 1))
                mean_var("hvar_ready")
                dve.wait_ge(s("hstd_ready"), l + 1)
                link(dve.reciprocal(cols[:, 2, :], cols[:, 1, :]))
                dve.wait_ge(s("h_kept"), NT * (l + 1))
                dve.wait_ge(s("gamma_loaded"), 32 * (l + 1))
                with dve.Fori(0, NT // UNR) as g:
                    do.turn()
                    tiles = [(t, acc[:, bass.ds(t, 1), 0:D]) for t in (g * UNR + k for k in range(UNR))]
                    do.link_all(dve.scalar_tensor_tensor(out=ht, in0=ht, scalar=mean[:, bass.ds(t, 1)], in1=gam.unsqueeze(1),
                                                         op0=ALU.subtract, op1=ALU.mult) for t, ht in tiles)
                    for t, ht in tiles:
                        dve.scalar_tensor_tensor(out=ht, in0=ht, scalar=cols[:, 2, bass.ds(t, 1)], in1=bet.unsqueeze(1),
                                                 op0=ALU.mult, op1=ALU.add).then_inc(s("z_ready"), 1)
                if l == 0:
                    dve.wait_ge(s("silu_done"), NT)
            dve.wait_ge(s("x_tile_used"), NT)
            with dve.Fori(0, NT // UNR) as g:
                do.turn()
                tiles = [(t, nodes[:, bass.ds(t, 1), :]) for t in (g * UNR + k for k in range(UNR))]
                dve.wait_ge(s("silu_done"), g * UNR + (NT + UNR))
                do.link_all(dve.tensor_tensor(nt, acc[:, bass.ds(t, 1), 0:D], mixo[:, bass.ds(t, 1), :], ALU.add) for t, nt in tiles)
                dve.sem_inc(s("x2_summed"), UNR)
                do.link_all(dve.bn_stats(lnst[:, bass.ds(t, 1), :], nt) for t, nt in tiles)
            mean_var("yvar_ready")

            dve.wait_ge(s("b_out_loaded"), 16)
            link(dve.tensor_scalar(inv_temp[:, :], inv_temp[:, :], 0.1, 5.0, ALU.max, ALU.min))
            link(dve.reciprocal(inv_temp[:, :], inv_temp[:, :]))
            split3(gbias3[0][:, :], brow[:, 0, :], D)
            heads = lambda ap: ap.rearrange("p (h g) -> p h g", g=G)
            dve.wait_ge(s("wc_made"), 1)
            for k in range(2):
                for r in range(2):
                    link(dve.tensor_tensor(heads(wc[:, k, :])[:, r:H:2, :], heads(ps[:, 4 + 2 * r + k, :])[:, r:H:2, :],
                                           inv_temp[:, r:H:2].unsqueeze(2).to_broadcast([P, H // 2, G]), ALU.mult))
            dve.wait_ge(s("lb_made"), 1)
            lb = split[:, 0, 0:HG]
            link(dve.tensor_tensor(heads(lb), heads(ps[0:3, 3, :]), b_sl[:, :].unsqueeze(1).to_broadcast([3, H, G]), ALU.add))
            link(dve.tensor_tensor(heads(split[:, 1, 0:HG]), heads(lb), inv_temp[0:3, :].unsqueeze(2).to_broadcast([3, H, G]), ALU.mult))
            link(dve.tensor_copy(lbrow, split[:, 1, 0:HG]))
            split3(lbias3[:, :], lbrow, HG)
            dve.sem_inc(s("wc_ready"), 1)
            dve.wait_ge(s("ystd_ready"), 1)
            link(dve.reciprocal(c2, c1))
            dve.wait_ge(s("x2_stored"), 80)

            def slice_step(i, par):
                t = live(i, 0)
                if t is not None:
                    if not isinstance(t, int) or t >= 2:
                        dve.wait_ge(s("xl_turned"), t - 1)
                        dve.wait_ge(s("xl_copied"), t - 1)
                    dve.tensor_scalar(xl_ring[:, par:par + 1, :], nodes[:, bass.ds(t, 1), :], mean[:, bass.ds(t, 1)], cols[:, 2, bass.ds(t, 1)],
                                      ALU.subtract, ALU.mult).then_inc(s("xl_ready"), 1)
                t = live(i, 1)
                if t is not None:
                    q = 1 - par
                    dve.wait_ge(s("logits_made"), t + 1)
                    link(dve.tensor_reduce(head8[:, q, 0, :], heads(ps[0:PT, 4 + q, :]), AX.X, ALU.max))
                    dve.tensor_tensor(heads(ex_ring[:, q, :]), heads(ps[0:PT, 4 + q, :]), head8[:, q, 0, :].unsqueeze(2).to_broadcast([PT, H, G]),
                                      ALU.subtract).then_inc(s("shifted"), 1)
                t = live(i, 2)
                if t is not None:
                    dve.wait_ge(s("exp_done"), t + 1)
                    w = heads(ex_ring[:, par, :])
                    link(dve.tensor_reduce(head8[:, par, 1, :], w, AX.X, ALU.add))
                    link(dve.reciprocal(head8[:, par, 2, :], head8[:, par, 1, :]))
                    if not isinstance(t, int) or t >= 2:
                        dve.wait_ge(s("w_used"), t - 1)
                        dve.wait_ge(s("w_kept"), t - 1)
                    dve.tensor_tensor(heads(w_ring[:, par, :]), w, head8[:, par, 2, :].unsqueeze(2).to_broadcast([PT, H, G]), ALU.mult).then_inc(s("w_ready"), 1)
            run_tiles(dve, do, slice_step, NT, 2)

            dve.wait_ge(s("slices_summed"), 1)
            dve.wait_ge(s("w_kept"), NT)
            link(dve.tensor_scalar(rb[:, 0, :], ps[:, 0:4, D:D + 1].rearrange("p a b -> p (a b)"), 1e-5, None, ALU.add))
            link(dve.reciprocal(rb[:, 1, :], rb[:, 0, :]))
            for j in range(4):
                link(dve.tensor_scalar(tok[:, j, :], ps[:, j, 0:257], rb[:, 1, j:j + 1], None, ALU.mult))
            dve.sem_inc(s("tok_ready"), 1)
            dve.wait_ge(s("stok_made"), 1)
            dve.memset(osT, 0.0).then_inc(s("osT_zeroed"), 1)
            dve.wait_ge(s("scores_made"), 1)
            mx = head8[0:HD, 0, 0, :]
            link(dve.tensor_reduce(mx, heads(ps[0:HD, 4, :]), AX.X, ALU.max))
            dve.tensor_tensor(heads(attn), heads(ps[0:HD, 4, :]), mx.unsqueeze(2).to_broadcast([HD, H, G]), ALU.subtract).then_inc(s("scores_shifted"), 1)
            dve.wait_ge(s("scores_exp"), 1)
            link(dve.tensor_reduce(head8[0:HD, 0, 1, :], heads(attn), AX.X, ALU.add))
            link(dve.reciprocal(head8[0:HD, 0, 2, :], head8[0:HD, 0, 1, :]))
            dve.tensor_tensor(heads(attn), heads(attn), head8[0:HD, 0, 2, :].unsqueeze(2).to_broadcast([HD, H, G]), ALU.mult).then_inc(s("attn_ready"), 1)

            dve.wait_ge(s("x2_back"), 80)
            def out_step(i, par):
                t = live(i, 1)
                if t is not None:
                    q = 1 - par
                    dve.wait_ge(s("y_made"), t + 1)
                    xt = nodes[:, bass.ds(t, 1), :]
                    dve.tensor_tensor(xt, ps[0:PT, 4 + q, 0:D].unsqueeze(1), xt, ALU.add).then_inc(s("out_ready"), 1)
            run_tiles(dve, None, out_step, NT, 1)


def kernel(**inputs):
    import numpy as _np
    import concourse.bacc as _bacc
    from concourse import mybir as _mybir
    from concourse.bass_utils import run_bass_kernel_spmd as _run

    nc = _bacc.Bacc("TRN2", target_bir_lowering=False, num_devices=1)
    arrays, args = {}, {}
    for name, value in inputs.items():
        value = _np.ascontiguousarray(value)
        arrays[f"in_{name}_dram"] = value
        args[name] = nc.dram_tensor(f"in_{name}_dram", value.shape, _mybir.dt.from_np(value.dtype), kind="ExternalInput").ap()
    out = nc.dram_tensor("out_0_dram", (N, D), _mybir.dt.float32, kind="ExternalOutput").ap()
    gps_kernel(nc, args, out)
    r = _run(nc, [arrays], core_ids=[0])
    return r.results[0]["out_0_dram"]
```
